# Optimizing a Trainium2 kernel written in Bass

```python
import numpy as np
import jax
import jax.numpy as jnp

def _softmax(x, axis=-1):
    return jax.nn.softmax(x, axis=axis)

def _gelu(x):
    return jax.nn.gelu(x, approximate=True)

def _silu(x):
    return jax.nn.silu(x)

def _sigmoid(x):
    return jax.nn.sigmoid(x)

def _layernorm(x, axis=-1, eps=1e-05):
    m = jnp.mean(x, axis=axis, keepdims=True)
    v = jnp.var(x, axis=axis, keepdims=True)
    return (x - m) / jnp.sqrt(v + eps)

def _scatter_add(tgt, idx, src, axis=0):
    return tgt.at[idx].add(src)

def _segment_sum(src, seg, n):
    return jax.ops.segment_sum(src, seg, n)
kernel_name = 'mk_gnn_ffn_d1_gnn_r8_0d09bc'

def setup_inputs(seed: int=0):
    np.random.seed(seed)
    _w = jnp.asarray

    def _rec_inputs():
        import jax
        import jax.numpy as jnp
        _gk = jax.random.key(seed)
        x = -0.000125 + 0.9999 * jax.random.normal(jax.random.fold_in(_gk, 1), (8192, 512), jnp.float32)
        src = jax.random.randint(jax.random.fold_in(_gk, 2), (131072,), 0, 8192, jnp.int32)
        dst = jax.random.randint(jax.random.fold_in(_gk, 3), (131072,), 0, 8192, jnp.int32)
        _o = jnp.argsort(dst, stable=True)
        src = src[_o]
        dst = dst[_o]
        edge_weight = jax.random.uniform(jax.random.fold_in(_gk, 12), (131072,), jnp.float32, 0.0, 0.999998)
        return (x, src, dst, edge_weight)
    x, src, dst, edge_weight = _rec_inputs()

    def _L0_gnn_setup():
        import jax, jax.numpy as jnp
        import numpy as np
        N_NODES = 8192
        N_EDGES = 65536
        FEAT_DIM = 512
        EMBED_DIM = 512
        key = jax.random.key(seed)
        k1, k2, k3, k4, k5 = jax.random.split(key, 5)
        x = jax.random.normal(k1, (N_NODES, FEAT_DIM), dtype=jnp.float32)
        limit = float(np.sqrt(6.0 / (EMBED_DIM + FEAT_DIM)))
        weight = jax.random.uniform(k2, (EMBED_DIM, FEAT_DIM), dtype=jnp.float32, minval=-limit, maxval=limit)
        row = jax.random.randint(k3, (N_EDGES,), 0, N_NODES, dtype=jnp.int64)
        col = jax.random.randint(k4, (N_EDGES,), 0, N_NODES, dtype=jnp.int64)
        vals = jax.random.uniform(k5, (N_EDGES,), dtype=jnp.float32)
        return {'x': x, 'weight': weight, 'row': row, 'col': col, 'vals': vals}
    _L0_gnn_all = _L0_gnn_setup()
    _L0_gnn_in = {k: v for k, v in _L0_gnn_all.items() if k in ('weight',)}
    del _L0_gnn_all

    def _L0_ffn_setup():
        import jax, jax.numpy as jnp
        import numpy as np
        MARK_AX = 0
        OP_MUL = 1
        OPCODE_BASE = 2
        ALU_LO, ALU_HI = (64, 80)
        AX_CARRY_LO, AX_CARRY_HI = (96, 112)
        OUTPUT_LO, OUTPUT_HI = (128, 144)
        NIB_A, NIB_B, RESULT, OP_START = (0, 1, 2, 3)
        GE_DIM = 160
        N_POS = 8
        N_LAYERS = 7
        OPCODE = 27

        def _decode_nibble(x16):
            return jnp.argmax(x16 > 0.5, axis=-1).astype(x16.dtype)
        key = jax.random.key(seed)
        k1, k2, k3 = jax.random.split(key, 3)
        x_bd = jax.random.uniform(k1, (4, 1024, 512), dtype=jnp.float32)
        W = jax.random.normal(k2, (N_LAYERS, GE_DIM, GE_DIM), dtype=jnp.float32) * 0.05
        b = jax.random.normal(k3, (N_LAYERS, GE_DIM), dtype=jnp.float32) * 0.01
        return {'x_bd': x_bd, 'W': W, 'b': b}
    _L0_ffn_all = _L0_ffn_setup()
    _L0_ffn_in = {k: v for k, v in _L0_ffn_all.items() if k in ('W', 'b')}
    del _L0_ffn_all
    return {'x': x, 'src': src, 'dst': dst, 'edge_weight': edge_weight, 'L0_gnn_weight': _L0_gnn_in['weight'], 'L0_ffn_W': _L0_ffn_in['W'], 'L0_ffn_b': _L0_ffn_in['b']}

def reference(x, src, dst, edge_weight, L0_gnn_weight, L0_ffn_W, L0_ffn_b):
    import jax
    import jax.numpy as jnp

    def _L0_gnn_ref(x, weight, row, col, vals):
        import jax, jax.numpy as jnp
        import numpy as np
        N_NODES = 8192
        N_EDGES = 65536
        FEAT_DIM = 512
        EMBED_DIM = 512
        h = jnp.einsum('nf,ef->ne', x, weight)
        msgs = vals[:, None] * h[col]
        out = jax.ops.segment_sum(msgs, row, num_segments=N_NODES)
        return out

    def _L0_ffn_ref(x_bd, W, b):
        import jax, jax.numpy as jnp
        import numpy as np
        MARK_AX = 0
        OP_MUL = 1
        OPCODE_BASE = 2
        ALU_LO, ALU_HI = (64, 80)
        AX_CARRY_LO, AX_CARRY_HI = (96, 112)
        OUTPUT_LO, OUTPUT_HI = (128, 144)
        NIB_A, NIB_B, RESULT, OP_START = (0, 1, 2, 3)
        GE_DIM = 160
        N_POS = 8
        N_LAYERS = 7
        OPCODE = 27

        def _decode_nibble(x16):
            return jnp.argmax(x16 > 0.5, axis=-1).astype(x16.dtype)
        B, S, D = x_bd.shape
        mask = (x_bd[..., MARK_AX] >= 0.5) & (x_bd[..., OP_MUL] >= 0.5)
        a_lo = _decode_nibble(x_bd[..., ALU_LO:ALU_LO + 16])
        a_hi = _decode_nibble(x_bd[..., ALU_HI:ALU_HI + 16])
        b_lo = _decode_nibble(x_bd[..., AX_CARRY_LO:AX_CARRY_LO + 16])
        b_hi = _decode_nibble(x_bd[..., AX_CARRY_HI:AX_CARRY_HI + 16])
        op_val = x_bd[..., OPCODE_BASE + OPCODE]
        x_ge = jnp.zeros((B, S, N_POS, GE_DIM), dtype=x_bd.dtype)
        x_ge = x_ge.at[..., 0, NIB_A].set(a_lo)
        x_ge = x_ge.at[..., 1, NIB_A].set(a_hi)
        x_ge = x_ge.at[..., 0, NIB_B].set(b_lo)
        x_ge = x_ge.at[..., 1, NIB_B].set(b_hi)
        x_ge = x_ge.at[..., :, OP_START + OPCODE].set(op_val[..., None])
        h = x_ge
        for i in range(N_LAYERS):
            h = jnp.einsum('bspd,ed->bspe', h, W[i]) + b[i]
            if i < N_LAYERS - 1:
                h = jax.nn.relu(h)
        res_lo = jnp.clip(jnp.round(h[..., 0, RESULT]), 0, 15).astype(jnp.int32)
        res_hi = jnp.clip(jnp.round(h[..., 1, RESULT]), 0, 15).astype(jnp.int32)
        m = mask[..., None].astype(x_bd.dtype)
        add_lo = 2.0 * jax.nn.one_hot(res_lo, 16, dtype=x_bd.dtype) * m
        add_hi = 2.0 * jax.nn.one_hot(res_hi, 16, dtype=x_bd.dtype) * m
        out = x_bd.at[..., OUTPUT_LO:OUTPUT_LO + 16].add(add_lo)
        out = out.at[..., OUTPUT_HI:OUTPUT_HI + 16].add(add_hi)
        return out
    x = x + _L0_gnn_ref(_layernorm(x, axis=-1), L0_gnn_weight, src, dst, edge_weight)
    x = x + _L0_ffn_ref(_layernorm(x, axis=-1)[None], L0_ffn_W, L0_ffn_b)[0]
    return x

_drawn_inputs = setup_inputs


def setup_inputs(seed=0):
    import zlib

    import numpy as np

    out = dict(_drawn_inputs(seed))
    spreads = {}
    factors = {}
    for name, (base, spread) in spreads.items():
        noise = np.random.default_rng([zlib.crc32(name.encode()), seed]).standard_normal(out[name].shape)
        drawn = base * np.exp(spread * noise) if base else spread * noise
        out[name] = jnp.asarray(drawn.astype(out[name].dtype))
    for name, factor in factors.items():
        out[name] = (out[name] * factor).astype(out[name].dtype)
    return out
```

```python
from contextlib import ExitStack

import concourse.bass as bass
from concourse import mybir

F32 = mybir.dt.float32
F32R = mybir.dt.float32r
I32 = mybir.dt.int32
BF16 = mybir.dt.bfloat16
ALU = mybir.AluOpType
ACT = mybir.ActivationFunctionType
AX_X = mybir.AxisListType.X


def gnn_ffn(nc, x, src, dst, edge_weight, gnn_w, ffn_w, ffn_b, out):
    P = 128
    N, D = x.shape
    E = src.shape[0]
    T = N // P
    COLS = E // P
    CHUNKS = COLS + T
    BLK = 16
    ROWS = CHUNKS * P
    KD = D // P
    REC = 3
    Q = 8
    S_ITERS = COLS // (4 * Q)
    RING = 8
    PART = 4
    AGG = 4
    LOADS = 8
    L, G = ffn_w.shape[0], ffn_w.shape[1]
    REM = G - P
    NT = 4
    GRP = T // NT
    MARK_AX, OP_MUL, OPVAL = 0, 1, 2 + 27
    IN_A, IN_B, IN_OP, RESULT = 0, 1, 3 + 27, 2
    NIB0, OUT0 = 64, 128
    EPS = 1e-5
    MAGIC = float(3 << 22)
    ZW = 272
    assert CHUNKS % (2 * BLK) == 0 and S_ITERS * 2 == T and REM == 32

    ctx = ExitStack()
    with ctx:
        def sb(name, shape, dt=F32):
            return ctx.enter_context(nc.sbuf_tensor(name, shape, dt))

        def sem(name):
            return ctx.enter_context(nc.semaphore(name))

        h_dram = nc.dram_tensor("h_rows", [N, D], F32, kind="Internal").ap()
        rec_dram = nc.dram_tensor("edge_records", [ROWS, REC], F32, kind="Internal").ap()

        x1 = sb("x1", [P, T, D])
        REGION = 12544
        region = sb("region", [P, REGION])
        at = [0]

        def carve(n, dt=F32):
            at[0] += n
            assert at[0] <= REGION, at[0]
            v = region[:, at[0] - n:at[0]]
            return v if dt == F32 else v.bitcast(dt)

        src_i = carve(COLS, I32)
        dst_i = carve(COLS, I32)
        weight = carve(COLS)
        tile_f = carve(COLS)
        local_i = carve(COLS, I32)
        w_load = carve(KD * D).rearrange("p (k f) -> p k f", k=KD)
        wT = carve(KD * D).rearrange("p (k f) -> p k f", k=KD)
        tail = carve(4 * D)
        xn = tail[:, 0:D]
        xnT = tail[:, D:2 * D].rearrange("p (k n) -> p k n", k=KD)
        h_out = tail[:, 2 * D:4 * D].rearrange("p (s f) -> p s f", s=2)
        junk = tail[:, 0:COLS].bitcast(BF16).rearrange("p (s t) -> p s t", s=2)
        is_first = tail[0:T, 0:CHUNKS]
        iota_c = carve(CHUNKS)[0:T, :]
        src_f = h_out.rearrange("p s f -> p (s f)")
        tile_i = w_load.rearrange("p k f -> p (k f)")[:, 0:COLS].bitcast(I32)
        gathered = region[:, 0:RING * D].rearrange("p (s f) -> p s f", s=RING)
        hi = sb("hi", [P, PART, D], F32R)
        lo = sb("lo", [P, PART, D], F32R)
        onehot = sb("onehot", [P, PART, P], F32R)

        at[0] = RING * D
        LH = L - 2
        fw_load = carve(LH * G).rearrange("p (l d) -> p l d", l=LH)
        fw_load_r = carve(LH * G)[0:REM, :].rearrange("p (l d) -> p l d", l=LH)
        fwT = carve(LH * G).rearrange("p (l e) -> p l e", l=LH)
        fwT_r = carve(LH * G)[0:2 * REM, :].rearrange("p (l e) -> p l e", l=LH)
        fw_in = carve(2 * G)[0:5, :].rearrange("p (s e) -> p s e", s=2)
        act_m = carve(4 * NT * P).rearrange("p (b s n) -> p b s n", b=2, s=2)
        act_r = carve(2 * NT * P)[0:2 * REM, :].rearrange("p (b n) -> p b n", b=2)
        feat = carve(NT * P)[0:5, :]
        nib = carve(NT * 4 * 16).rearrange("p (t g j) -> p t g j", t=NT, g=4)
        rev16 = carve(NT * 4 * 16).rearrange("p (t g j) -> p t g j", t=NT, g=4)
        hot = carve(NT * 2 * 16).rearrange("p (t s j) -> p t s j", t=NT, s=2)
        xn_f = region[:, 0:2 * NT * D].rearrange("p (b t f) -> p b t f", b=2, t=NT)

        iota_t = sb("iota_t", [P, T])
        iota_p = sb("iota_p", [P, P])
        ident = sb("ident", [P, P])
        before = sb("before", [P, P])
        ones = sb("ones", [P, P])
        zeros = sb("zeros", [P, ZW])
        below = sb("below", [P, T + 1])
        count = sb("count", [P, T])
        counter = sb("counter", [P, 2, T])
        hit = sb("hit", [P, 2, T])
        tot_i = sb("tot_i", [T, 2], I32)
        n_chunks = sb("n_chunks", [T, 2])
        first = sb("first", [T, 1])
        first_diag = sb("first_diag", [T, T])
        flags = sb("flags", [1, CHUNKS + 8], I32)
        rank_f = sb("rank_f", [P, 4 * Q])
        rank_i = sb("rank_i", [P, 4 * Q], I32)
        row_a = sb("row_a", [P, 4 * Q], I32)
        row_b = sb("row_b", [P, 4 * Q], I32)
        row_c = sb("row_c", [P, 4 * Q], I32)
        row = sb("row", [P, 4 * Q], I32)
        rec = sb("rec", [P, 4 * Q, REC])
        stats = sb("stats", [P, 6])
        mv = sb("mv", [P, 2])
        sd = sb("sd", [P, 1])
        rstd = sb("rstd", [P, 1])
        eps = sb("eps", [P, 1])
        meta = sb("meta", [P, 2, BLK, REC])
        f_stats = sb("f_stats", [P, NT, 6])
        f_mv = sb("f_mv", [P, NT, 2])
        f_sd = sb("f_sd", [P, NT])
        f_rstd = sb("f_rstd", [P, NT])
        f_mask = sb("f_mask", [P, 2, NT])
        f_top = sb("f_top", [P, NT, 4])
        f_val = sb("f_val", [P, NT, 4])
        f_in = sb("f_in", [P, NT, 5])
        f_res = sb("f_res", [P, 2, NT * 2])
        bias = sb("bias", [P, L - 1])
        bias_r = sb("bias_r", [2 * REM, L - 1])
        fw_out = sb("fw_out", [P, 1])
        fw_out_r = sb("fw_out_r", [2 * REM, 1])
        b_out = sb("b_out", [P, 1])

        psum = ctx.enter_context(nc.psum_tensor("psum", [P, 8 * D], F32))

        def bank(i, n=1):
            return psum[:, i * D:(i + n) * D]

        s_src, s_dst, s_wt, s_w = sem("src_loaded"), sem("dst_loaded"), sem("weight_loaded"), sem("w_loaded")
        s_x = [sem(f"x_loaded{i}") for i in range(LOADS)]
        s_fill = sem("records_cleared")
        s_const = sem("constants")
        s_v = sem("vector_steps")
        s_cnt = sem("counted")
        s_tot = sem("totals")
        s_nch = sem("chunks_per_tile")
        s_first = sem("first_chunks")
        s_diag = sem("first_diag_ready")
        s_base = sem("group_bases")
        s_isf = sem("is_first_ready")
        s_flagm = sem("flags_summed")
        s_flags = sem("flags_ready")
        s_wtr, s_wev = sem("w_transposed"), sem("w_evacuated")
        s_split = sem("edges_split")
        s_rank = sem("rank_steps")
        s_row = sem("rows_ready")
        s_rec = sem("records_ready")
        s_scat = [sem(f"scattered{q}") for q in range(4)]
        s_var, s_sd, s_xn = sem("variance"), sem("deviation"), sem("normalised")
        s_tr, s_tev, s_mm, s_hev = sem("transposed"), sem("xnT_ready"), sem("multiplied"), sem("h_evacuated")
        s_hst = [sem(f"h_stored{u}") for u in range(2)]
        s_meta = [sem(f"meta_loaded{u}") for u in range(2)]
        s_gat = [sem(f"rows_gathered{k}") for k in range(RING)]
        s_hi = sem("hi_ready")
        s_op = sem("operands_ready")
        s_done = sem("chunks_summed")
        s_aggfree = sem("agg_banks_free")
        s_x1 = sem("x1_ready")

        s_st = sem("ln_steps")
        s_conv = sem("row_steps")
        s_fw, s_fin, s_fb = sem("ffn_w_loaded"), sem("ffn_in_loaded"), sem("ffn_b_loaded")
        s_fz = sem("ffn_in_cleared")
        s_fwt, s_fwe = sem("ffn_w_transposed"), sem("ffn_w_evacuated")
        s_rev = sem("rev16_ready")
        s_ln = sem("ffn_ln_steps")
        s_fvar, s_fsd = sem("ffn_variance"), sem("ffn_deviation")
        s_feat, s_ftr, s_fte = sem("features_ready"), sem("features_transposed"), sem("features_evacuated")
        s_pr, s_p0, s_p1 = sem("rem_summed"), sem("main0_summed"), sem("main1_summed")
        s_ar, s_a0, s_a1 = sem("rem_ready"), sem("main0_ready"), sem("main1_ready")
        s_res, s_hot, s_y = sem("results_summed"), sem("one_hots_added"), sem("outputs_ready")
        s_out = [sem(f"stored{b}") for b in range(2)]

        block = ctx.enter_context(nc.Block())

        def wait_apart(eng, *waits):
            for _, register, step_by in waits:
                eng.reg_add(register, register, step_by)
            eng.wait_ge(s_const, 7)
            for semaphore, register, _ in waits:
                eng.wait_ge(semaphore, register)

        def counters(eng, *names):
            found = [ctx.enter_context(eng.register(name)) for name in names]
            for register in found:
                eng.reg_mov(register, 0)
            return found

        @block.sync
        def _(sp):
            sp.dma_start(src_i, src.rearrange("(p t) -> p t", p=P)).then_inc(s_src, 16)
            sp.dma_start(dst_i, dst.rearrange("(p t) -> p t", p=P)).then_inc(s_dst, 16)
            sp.dma_start(weight, edge_weight.rearrange("(p t) -> p t", p=P)).then_inc(s_wt, 16)
            for i in range(LOADS):
                n = T // LOADS
                sp.dma_start(x1[:, i * n:(i + 1) * n, :],
                             x[i * n * P:(i + 1) * n * P, :].rearrange("(t p) f -> p t f", p=P)).then_inc(s_x[i], 16)
            sp.wait_ge(s_const, 7)
            for i in range(ROWS * REC // P // ZW):
                sp.dma_start(rec_dram.rearrange("(p r) c -> p (r c)", p=P)[:, i * ZW:(i + 1) * ZW],
                             zeros[:, :]).then_inc(s_fill, 16)
            sp.wait_ge(s_split, 4)
            sp.dma_start(w_load, gnn_w.rearrange("(k p) f -> p k f", p=P)).then_inc(s_w, 16)
            with sp.Fori(0, S_ITERS) as it:
                for u in range(2):
                    sp.wait_ge(s_hev, it * 2 + (u + 1))
                    sp.dma_start(h_dram[bass.ds((it * 2 + u) * P, P), :], h_out[:, u, :]).then_inc(s_hst[u], 16)
            for q in range(4):
                sp.wait_ge(s_scat[q], 16 * Q * S_ITERS)
            rec_v = rec_dram.rearrange("(b p k) c -> p b (k c)", p=P, k=BLK)
            for u in range(2):
                sp.dma_start(meta[:, u, :, :].rearrange("p k c -> p (k c)"), rec_v[:, u, :]).then_inc(s_meta[u], 16)
            sp.wait_ge(s_fz, 1)
            sp.dma_start(fw_load, ffn_w[1:L - 1, 0:P, :].rearrange("l e d -> e l d")).then_inc(s_fw, 16)
            sp.dma_start(fw_load_r, ffn_w[1:L - 1, P:G, :].rearrange("l e d -> e l d")).then_inc(s_fw, 16)
            with nc.allow_non_contiguous_dma(reason="columns of the first layer, and the biases: a few hundred words"):
                for r, s, c in ((0, 0, IN_A), (2, 0, IN_B), (4, 0, IN_OP), (1, 1, IN_A), (3, 1, IN_B), (4, 1, IN_OP)):
                    sp.dma_start(fw_in[r:r + 1, s, :], ffn_w[0:1, :, c]).then_inc(s_fin, 16)
                sp.dma_start(bias[:, :], ffn_b[0:L - 1, 0:P].rearrange("l e -> e l")).then_inc(s_fb, 16)
                for s in range(2):
                    sp.dma_start(bias_r[s * REM:(s + 1) * REM, :],
                                 ffn_b[0:L - 1, P:G].rearrange("l e -> e l")).then_inc(s_fb, 16)
                    sp.dma_start(fw_out_r[s * REM:(s + 1) * REM, :],
                                 ffn_w[L - 1, RESULT:RESULT + 1, P:G].rearrange("a e -> e a")).then_inc(s_fb, 16)
                sp.dma_start(fw_out[:, :], ffn_w[L - 1, RESULT:RESULT + 1, 0:P].rearrange("a e -> e a")).then_inc(s_fb, 16)
                sp.dma_start(b_out[:, :], ffn_b[L - 1:L, RESULT:RESULT + 1].to_broadcast([P, 1])).then_inc(s_fb, 16)
            with sp.Fori(1, CHUNKS // (2 * BLK)) as it:
                for u in range(2):
                    sp.wait_ge(s_op, it * (2 * BLK) + (RING + (u - 1) * BLK))
                    sp.dma_start(meta[:, u, :, :].rearrange("p k c -> p (k c)"),
                                 rec_v[:, bass.ds(it * 2 + u, 1), :]).then_inc(s_meta[u], 16)
            with sp.Fori(0, GRP // 2) as it:
                for b in range(2):
                    sp.wait_ge(s_y, it * 2 + (b + 1))
                    sp.dma_start(out[bass.ds((it * 2 + b) * NT * P, NT * P), :].rearrange("(t p) f -> p t f", p=P),
                                 xn_f[:, b, :, :]).then_inc(s_out[b], 16)
            for b in range(2):
                sp.wait_ge(s_out[b], 16 * (GRP // 2))

        @block.gpsimd
        def _(pool):
            pool.memset(zeros[:, :], 0.0).then_inc(s_const, 1)
            pool.iota(iota_t[:, :], [[1, T]], base=0, channel_multiplier=0,
                      allow_small_or_imprecise_dtypes=True).then_inc(s_const, 1)
            pool.iota(iota_p[:, :], [[1, P]], base=0, channel_multiplier=0,
                      allow_small_or_imprecise_dtypes=True).then_inc(s_const, 1)
            pool.iota(iota_c, [[1, CHUNKS]], base=0, channel_multiplier=0,
                      allow_small_or_imprecise_dtypes=True).then_inc(s_const, 1)
            pool.memset(ones[:, :], 1.0).then_inc(s_const, 1)
            pool.wait_ge(s_const, 5)
            pool.affine_select(out=before[:, :], in_=ones[:, :], compare_op=ALU.is_gt, fill=0.0, base=0,
                               pattern=[[1, P]], channel_multiplier=-1).then_inc(s_const, 1)
            pool.affine_select(out=ident[:, :], in_=ones[:, :], compare_op=ALU.is_equal, fill=0.0, base=0,
                               pattern=[[1, P]], channel_multiplier=-1).then_inc(s_const, 1)
            pool.wait_ge(s_fill, 16 * (ROWS * REC // P // ZW))
            quarters, quarters_too = counters(pool, "rows_wanted", "records_wanted")
            with pool.Fori(0, S_ITERS):
                for q in range(4):
                    wait_apart(pool, (s_row, quarters, 1), (s_rec, quarters_too, 1))
                    for j in range(q * Q, q * Q + Q):
                        pool.indirect_dma_start(rec_dram, bass.IndirectOffsetOnAxis(ap=row[:, j:j + 1], axis=0),
                                                rec[:, j, :], None).then_inc(s_scat[q], 16)
            for u in range(2):
                pool.wait_ge(s_hst[u], 16 * S_ITERS)
            slots, *blocks = counters(pool, "slots_wanted", "even_block_wanted", "odd_block_wanted")
            with pool.Fori(0, CHUNKS // (2 * BLK)):
                for u in range(2):
                    for j in range(BLK):
                        loaded = [(s_meta[u], blocks[u], 16)] if j == 0 else []
                        wait_apart(pool, (s_op, slots, 1), *loaded)
                        pool.indirect_dma_start(
                            gathered[:, j % RING, :], None, h_dram,
                            bass.IndirectOffsetOnAxis(ap=meta[:, u, j, 0:1].bitcast(I32), axis=0),
                        ).then_inc(s_gat[j % RING], 16)

            pool.wait_ge(s_fwe, 1)
            pool.iota(rev16.rearrange("p t g j -> p (t g) j"), [[0, NT * 4], [-1, 16]], base=16, channel_multiplier=0,
                      allow_small_or_imprecise_dtypes=True).then_inc(s_rev, 1)
            with pool.Fori(0, GRP // 2) as it:
                for b in range(2):
                    pool.wait_ge(s_hot, it * 2 + (b + 1))
                    pool.tensor_tensor(xn_f[:, b, :, :], xn_f[:, b, :, :], x1[:, bass.ds((it * 2 + b) * NT, NT), :],
                                       ALU.add).then_inc(s_y, 1)

        @block.scalar
        def _(act):
            act.preload_act_table(ACT.Sqrt)
            for k in range(KD):
                act.wait_ge(s_wtr, k + 1)
                act.activation(wT[:, k, :], bank(k), ACT.Copy).then_inc(s_wev, 1)
            act.wait_ge(s_split, 4)
            act.wait_ge(s_dst, 16)
            act.wait_ge(s_wt, 16)
            with act.Fori(0, S_ITERS) as it:
                for u in range(2):
                    for q in (2 * u, 2 * u + 1):
                        act.wait_ge(s_scat[q], it * (16 * Q))
                        c = bass.ds((it * 4 + q) * Q, Q)
                        r = rec[:, q * Q:(q + 1) * Q, :]
                        act.activation(r[:, :, 0].bitcast(I32), dst_i[:, c], ACT.Copy)
                        act.activation(r[:, :, 1], local_i[:, c], ACT.Copy)
                        act.activation(r[:, :, 2], weight[:, c], ACT.Copy).then_inc(s_rec, 1)
                    n = it * 2 + (u + 1)
                    act.wait_ge(s_var, n)
                    act.activation(sd[:, :], mv[:, 1:2], ACT.Sqrt, bias=eps[:, 0:1]).then_inc(s_sd, 1)
                    act.wait_ge(s_tr, n)
                    act.activation(xnT.rearrange("p k n -> p (k n)"), bank(4), ACT.Copy).then_inc(s_tev, 1)
                    act.wait_ge(s_mm, n)
                    act.wait_ge(s_hst[u], it * 16)
                    act.activation(h_out[:, u, :], bank(5), ACT.Copy).then_inc(s_hev, 1)
            act.wait_ge(s_fwt, 1)
            for l in range(LH):
                act.activation(fwT[:, l, :], psum[:, l * 512:l * 512 + G], ACT.Copy)
                act.activation(fwT_r[0:REM, l, :], psum[0:REM, l * 512 + 256:l * 512 + 256 + G], ACT.Copy)
                last = act.activation(fwT_r[REM:2 * REM, l, :], psum[0:REM, l * 512 + 256:l * 512 + 256 + G], ACT.Copy)
            last.then_inc(s_fwe, 1)
            with act.Fori(0, CHUNKS // RING) as it:
                for k in range(RING):
                    b = (it // 2) % 2
                    w = meta[:, bass.ds(b, 1), bass.ds((it % 2) * RING + k, 1), 2]
                    act.wait_ge(s_gat[k], it * 16 + 16)
                    act.wait_ge(s_done, it * RING + (k + 1))
                    act.activation(hi[:, k % PART, :], gathered[:, k, :], ACT.Copy,
                                   scale=w.rearrange("p a b -> p (a b)")).then_inc(s_hi, 1)
            act.wait_ge(s_fb, 16 * 7)
            with act.Fori(0, GRP // 2) as it:
                for b in range(2):
                    g = it * 2 + b
                    act.wait_ge(s_fvar, g + 1)
                    act.activation(f_sd[:, :], f_mv[:, :, 1], ACT.Sqrt, bias=eps[:, 0:1]).then_inc(s_fsd, 1)
                    act.wait_ge(s_ftr, g + 1)
                    act.activation(feat, bank(6)[0:5, :], ACT.Copy).then_inc(s_fte, 1)
                    for l in range(L - 1):
                        act.wait_ge(s_pr, g * (L - 1) + (l + 1))
                        act.activation(act_r[:, l % 2, :], bank(3 * (l % 2) + 2)[0:2 * REM, :], ACT.Relu,
                                       bias=bias_r[:, l:l + 1]).then_inc(s_ar, 1)
                        act.wait_ge(s_p0, g * (L - 1) + (l + 1))
                        act.activation(act_m[:, l % 2, 0, :], bank(3 * (l % 2)), ACT.Relu,
                                       bias=bias[:, l:l + 1]).then_inc(s_a0, 1)

        @block.vector
        def _(dve):
            steps = [0]

            def step(ins):
                steps[0] += 1
                ins.then_inc(s_v, 1)
                dve.wait_ge(s_v, steps[0])

            dve.memset(eps[:, :], EPS)
            dve.memset(below[:, 0:1], 0.0)
            dve.memset(below[:, T:T + 1], float(COLS))
            step(dve.memset(flags[:, :], 0))
            dve.wait_ge(s_src, 16)
            dve.tensor_copy(src_f, src_i).then_inc(s_split, 1)
            dve.tensor_scalar(tile_i, src_i, 7, None, ALU.arith_shift_right).then_inc(s_split, 1)
            dve.tensor_scalar(local_i, src_i, P - 1, None, ALU.bitwise_and).then_inc(s_split, 1)
            dve.wait_ge(s_split, 2)
            dve.tensor_copy(tile_f, tile_i).then_inc(s_split, 1)
            for b in range(1, T):
                if b >= 3:
                    dve.wait_ge(s_cnt, b - 2)
                dve.tensor_scalar(junk[:, b % 2, :], src_f, float(b * P), None, ALU.is_lt, ALU.add,
                                  accum_out=below[:, b:b + 1]).then_inc(s_cnt, 1)
            dve.wait_ge(s_cnt, T - 1)
            dve.tensor_tensor(count[:, :], below[:, 1:T + 1], below[:, 0:T], ALU.subtract).then_inc(s_cnt, 1)
            dve.wait_ge(s_tot, 1)
            step(dve.tensor_scalar(tot_i[:, 0:1], bank(6)[0:T, 0:1], float(P - 1), None, ALU.add))
            step(dve.tensor_scalar(tot_i[:, 1:2], tot_i[:, 0:1], 7, None, ALU.arith_shift_right))
            dve.tensor_scalar(n_chunks[:, 0:1], tot_i[:, 1:2], 1.0, None, ALU.max).then_inc(s_nch, 1)
            dve.wait_ge(s_first, 1)
            step(dve.tensor_copy(first[:, :], bank(6)[0:T, 64:65]))
            dve.tensor_scalar(first_diag[:, :], ident[0:T, 0:T], first[:, 0:1], float(P),
                              ALU.mult, ALU.mult).then_inc(s_diag, 1)
            dve.tensor_scalar(is_first, iota_c, first[:, 0:1], None, ALU.is_equal).then_inc(s_isf, 1)
            dve.wait_ge(s_base, 1)
            step(dve.tensor_copy(counter[:, 0, :], bank(7)[:, 0:T]))
            dve.wait_ge(s_flagm, 1)
            dve.tensor_copy(flags[:, 2:CHUNKS + 1], psum[0:1, 1:CHUNKS]).then_inc(s_flags, 1)
            dve.wait_ge(s_flags, 1)
            dve.wait_ge(s_split, 4)
            for i in range(LOADS):
                dve.wait_ge(s_x[i], 16)

            ln_wanted, = counters(dve, "ln_steps_wanted")
            with dve.Fori(0, S_ITERS) as it:
                for u in range(2):
                    for q in (2 * u, 2 * u + 1):
                        for j in range(Q):
                            a, b = j % 2, 1 - j % 2
                            t = tile_f[:, bass.ds(it * (4 * Q) + (q * Q + j), 1)]
                            dve.wait_ge(s_rank, it * (8 * Q) + 2 * (q * Q + j))
                            dve.scalar_tensor_tensor(hit[:, a, :], iota_t[:, :], t, counter[:, a, :], ALU.is_equal,
                                                     ALU.mult, accum_out=rank_f[:, q * Q + j:q * Q + j + 1]
                                                     ).then_inc(s_rank, 1)
                            dve.scalar_tensor_tensor(counter[:, b, :], iota_t[:, :], t, counter[:, a, :],
                                                     ALU.is_equal, ALU.add).then_inc(s_rank, 1)
                        s = slice(q * Q, (q + 1) * Q)
                        dve.wait_ge(s_rank, it * (8 * Q) + 2 * (q + 1) * Q)
                        base = (it * 4 + q) * 5
                        dve.tensor_copy(rank_i[:, s], rank_f[:, s]).then_inc(s_conv, 1)
                        dve.wait_ge(s_conv, base + 1)
                        dve.tensor_scalar(row_a[:, s], rank_i[:, s], P - 1, 4, ALU.bitwise_and,
                                          ALU.logical_shift_left).then_inc(s_conv, 1)
                        dve.tensor_scalar(row_b[:, s], rank_i[:, s], 7, BLK - 1, ALU.arith_shift_right,
                                          ALU.bitwise_and).then_inc(s_conv, 1)
                        dve.tensor_scalar(row_c[:, s], rank_i[:, s], ~(BLK * P - 1), None,
                                          ALU.bitwise_and).then_inc(s_conv, 1)
                        dve.wait_ge(s_conv, base + 4)
                        dve.tensor_tensor(row_a[:, s], row_a[:, s], row_b[:, s], ALU.bitwise_or).then_inc(s_conv, 1)
                        dve.wait_ge(s_conv, base + 5)
                        dve.wait_ge(s_scat[q], it * (16 * Q))
                        dve.tensor_tensor(row[:, s], row_a[:, s], row_c[:, s], ALU.bitwise_or).then_inc(s_row, 1)
                    n = it * 2 + u
                    dve.bn_stats(stats[:, :], x1[:, bass.ds(n, 1), :].rearrange("p a f -> p (a f)")).then_inc(s_st, 1)
                    dve.reg_mov(ln_wanted, n * 2)
                    wait_apart(dve, (s_st, ln_wanted, 1))
                    dve.bn_aggr(mv[:, :], stats[:, :]).then_inc(s_var, 1)
                    dve.wait_ge(s_sd, n + 1)
                    dve.reciprocal(rstd[:, :], sd[:, :]).then_inc(s_st, 1)
                    dve.wait_ge(s_st, n * 2 + 2)
                    dve.wait_ge(s_tr, n)
                    dve.tensor_scalar(xn, x1[:, bass.ds(n, 1), :].rearrange("p a f -> p (a f)"), mv[:, 0:1],
                                      rstd[:, 0:1], ALU.subtract, ALU.mult).then_inc(s_xn, 1)
                    dve.wait_ge(s_xn, n + 1)

            dve.wait_ge(s_tr, T)
            dve.wait_ge(s_tev, T)
            dve.memset(hit[:, 0, 0:1], 0.0).then_inc(s_op, RING)
            dve.memset(hit[:, 1, 0:1], 0.0).then_inc(s_aggfree, AGG)
            dve.wait_ge(s_hst[0], 16 * S_ITERS)
            dve.wait_ge(s_hst[1], 16 * S_ITERS)
            dve.memset(fw_in, 0.0).then_inc(s_fz, 1)

            def add_tile(n):
                a = x1[:, bass.ds(n, 1), :].rearrange("p a f -> p (a f)")
                dve.tensor_tensor(a, psum[:, bass.ds((n % AGG) * D, D)], a, ALU.add).then_inc(s_aggfree, 1)

            with ExitStack() as regs:
                mark = [regs.enter_context(dve.register(f"vmark{k}")) for k in range(RING)]
                tile = regs.enter_context(dve.register("vtile"))
                dve.reg_mov(tile, 0)
                with dve.Fori(0, CHUNKS // RING) as it:
                    dve.reg_load(mark, flags[0:1, bass.ds(it * RING, RING)])
                    for k in range(RING):
                        c = it * RING + k
                        b, j = (it // 2) % 2, (it % 2) * RING + k
                        m = meta[:, bass.ds(b, 1), bass.ds(j, 1), :].rearrange("p a b c -> p (a b c)")
                        dve.wait_ge(s_hi, c + 1)
                        dve.wait_ge(s_done, c + 1)
                        dve.scalar_tensor_tensor(lo[:, k % PART, :], gathered[:, k, :], m[:, 2:3],
                                                 hi[:, k % PART, :].bitcast(F32), ALU.mult, ALU.subtract)
                        dve.tensor_scalar(onehot[:, k % PART, :], iota_p[:, :], m[:, 1:2], None,
                                          ALU.is_equal).then_inc(s_op, 1)
                        with dve.If_ne(mark[k], 0):
                            dve.wait_ge(s_done, c + (PART - 1))
                            add_tile(dve.snap(tile, min_val=0, max_val=T - 1))
                            dve.reg_add(tile, tile, 1)
                dve.reg_load(mark[0], flags[0:1, CHUNKS:CHUNKS + 1])
                dve.wait_ge(s_done, CHUNKS + PART)
                with dve.If_ne(mark[0], 0):
                    add_tile(dve.snap(tile, min_val=0, max_val=T - 1))
            a = x1[:, T - 1, :]
            dve.tensor_tensor(a, bank((T - 1) % AGG), a, ALU.add).then_inc(s_x1, 1)
            dve.wait_ge(s_x1, 1)

            dve.wait_ge(s_rev, 1)
            dve.wait_ge(s_fb, 16 * 7)
            with dve.Fori(0, GRP // 2) as it:
                for b in range(2):
                    g = it * 2 + b
                    xg = xn_f[:, b, :, :]
                    seq = [0]
                    STEPS = 16

                    def done(ins):
                        seq[0] += 1
                        ins.then_inc(s_ln, 1)
                        dve.wait_ge(s_ln, g * STEPS + seq[0])

                    for i in range(NT):
                        last = dve.bn_stats(f_stats[:, i, :], x1[:, bass.ds(g * NT + i, 1), :].rearrange("p a f -> p (a f)"))
                    seq[0] += 1
                    last.then_inc(s_ln, 1)
                    dve.reg_mov(ln_wanted, g * STEPS)
                    wait_apart(dve, (s_ln, ln_wanted, seq[0]))
                    for i in range(NT):
                        last = dve.bn_aggr(f_mv[:, i, :], f_stats[:, i, :])
                    last.then_inc(s_fvar, 1)
                    dve.wait_ge(s_fsd, g + 1)
                    done(dve.reciprocal(f_rstd[:, :], f_sd[:, :]))
                    dve.wait_ge(s_out[b], it * 16)
                    for i in range(NT):
                        last = dve.tensor_scalar(xg[:, i, :], x1[:, bass.ds(g * NT + i, 1), :].rearrange("p a f -> p (a f)"),
                                                 f_mv[:, i, 0:1], f_rstd[:, i:i + 1], ALU.subtract, ALU.mult)
                    done(last)
                    done(dve.scalar_tensor_tensor(nib.rearrange("p t g j -> p t (g j)"), xg[:, :, NIB0:NIB0 + 64], 0.5,
                                                  rev16.rearrange("p t g j -> p t (g j)"), ALU.is_gt, ALU.mult))
                    done(dve.tensor_reduce(f_top[:, :, :], nib, AX_X, ALU.max))
                    done(dve.tensor_scalar(f_val[:, :, :], f_top[:, :, :], -1.0, 16.0, ALU.mult, ALU.add))
                    dve.tensor_copy(f_in[:, :, 4:5], xg[:, :, OPVAL:OPVAL + 1])
                    dve.scalar_tensor_tensor(f_in[:, :, 0:4], f_top[:, :, :], 0.0, f_val[:, :, :], ALU.is_gt,
                                             ALU.mult).then_inc(s_feat, 1)
                    done(dve.tensor_scalar(f_mask[:, 0, :], xg[:, :, MARK_AX], 0.5, 2.0, ALU.is_ge, ALU.mult))
                    done(dve.scalar_tensor_tensor(f_mask[:, 1, :], xg[:, :, OP_MUL], 0.5, f_mask[:, 0, :],
                                                  ALU.is_ge, ALU.mult))
                    for l in range(L - 1):
                        dve.wait_ge(s_p1, g * (L - 1) + (l + 1))
                        dve.tensor_scalar(act_m[:, l % 2, 1, :], bank(3 * (l % 2) + 1), bias[:, l:l + 1], 0.0,
                                          ALU.add, ALU.max).then_inc(s_a1, 1)
                    dve.wait_ge(s_res, g + 1)
                    for s in range(2):
                        last = dve.tensor_scalar(f_res[:, 0, s:2 * NT:2], bank(7 - s)[:, 0:NT], b_out[:, 0:1], MAGIC,
                                                 ALU.add, ALU.add)
                    done(last)
                    done(dve.tensor_scalar(f_res[:, 1, :], f_res[:, 0, :], MAGIC, 0.0, ALU.subtract, ALU.max))
                    done(dve.tensor_scalar(f_res[:, 0, :], f_res[:, 1, :], 15.0, None, ALU.min))
                    done(dve.tensor_tensor(hot.rearrange("p t s j -> p (t s) j"),
                                           iota_p[:, 0:16].unsqueeze(1).to_broadcast([P, 2 * NT, 16]),
                                           f_res[:, 0, :].unsqueeze(2).to_broadcast([P, 2 * NT, 16]), ALU.is_equal))
                    done(dve.tensor_tensor(hot.rearrange("p t s j -> p t (s j)"), hot.rearrange("p t s j -> p t (s j)"),
                                           f_mask[:, 1, :].unsqueeze(2).to_broadcast([P, NT, 32]), ALU.mult))
                    dve.tensor_tensor(xg[:, :, OUT0:OUT0 + 32], xg[:, :, OUT0:OUT0 + 32],
                                      hot.rearrange("p t s j -> p t (s j)"), ALU.add).then_inc(s_hot, 1)
                    while seq[0] < STEPS - 1:
                        done(dve.tensor_copy(sd[:, 0:1], eps[:, 0:1]))
                    done(dve.tensor_copy(sd[:, 0:1], eps[:, 0:1]))

        @block.tensor
        def _(pe):
            pe.wait_ge(s_const, 7)
            pe.wait_ge(s_w, 16)
            for k in range(KD):
                for j in range(KD):
                    last = pe.transpose(bank(k)[:, j * P:(j + 1) * P], w_load[:, j, k * P:(k + 1) * P], ident[:, :])
                last.then_inc(s_wtr, 1)
            pe.wait_ge(s_cnt, T)
            pe.matmul(bank(6)[0:T, 0:1], count[:, :], ones[:, 0:1], start=True, stop=True).then_inc(s_tot, 1)
            pe.wait_ge(s_nch, 1)
            pe.matmul(bank(6)[0:T, 64:65], before[0:T, 0:T], n_chunks[:, 0:1], start=True, stop=True).then_inc(s_first, 1)
            pe.wait_ge(s_diag, 1)
            pe.matmul(bank(7)[:, 0:T], before[:, :], count[:, :], start=True, stop=False)
            pe.matmul(bank(7)[:, 0:T], ones[0:T, :], first_diag[:, :], start=False, stop=True).then_inc(s_base, 1)
            pe.wait_ge(s_isf, 1)
            pe.wait_ge(s_wev, KD)
            for c in range(0, CHUNKS, D):
                e = min(CHUNKS, c + D)
                last = pe.matmul(psum[0:1, c:e], ones[0:T, 0:1], is_first[:, c:e], start=True, stop=True)
            last.then_inc(s_flagm, 1)
            with pe.Fori(0, T) as n:
                pe.wait_ge(s_xn, n + 1)
                for k in range(KD):
                    last = pe.transpose(bank(4)[:, k * P:(k + 1) * P], xn[:, k * P:(k + 1) * P], ident[:, :])
                last.then_inc(s_tr, 1)
                pe.wait_ge(s_tev, n + 1)
                for k in range(KD):
                    last = pe.matmul(bank(5), xnT[:, k, :], wT[:, k, :], start=(k == 0), stop=(k == KD - 1))
                last.then_inc(s_mm, 1)
            pe.wait_ge(s_flags, 1)
            pe.wait_ge(s_hev, T)
            pe.wait_ge(s_fw, 32)
            for l in range(LH):
                o = l * 512
                pe.transpose(psum[:, o:o + P], fw_load[:, l, 0:P], ident[:, :])
                pe.transpose(psum[:, o + P:o + G], fw_load_r[:, l, 0:P], ident[0:REM, 0:REM])
                pe.transpose(psum[0:REM, o + 256:o + 256 + P], fw_load[:, l, P:G], ident[:, :])
                last = pe.transpose(psum[0:REM, o + 256 + P:o + 256 + G], fw_load_r[:, l, P:G], ident[0:REM, 0:REM])
            last.then_inc(s_fwt, 1)
            pe.wait_ge(s_fwe, 1)
            for i in range(2):
                last = pe.matmul(bank(0)[:, i * 256:(i + 1) * 256], ident[:, :], zeros[:, 0:256], start=(i == 0),
                                 stop=True, skip_group_check=True)
            last.then_inc(s_done, PART)
            with ExitStack() as regs:
                mark = [regs.enter_context(pe.register(f"pmark{k}")) for k in range(RING)]
                tile = regs.enter_context(pe.register("ptile"))
                at_bank = regs.enter_context(pe.register("pbank"))
                pe.reg_mov(tile, 0)
                pe.reg_mov(at_bank, 0)

                def summed():
                    return psum[:, bass.ds(pe.snap(at_bank, min_val=0, max_val=(AGG - 1) * D), D)]

                with pe.Fori(0, CHUNKS // RING) as it:
                    pe.reg_load(mark, flags[0:1, bass.ds(it * RING + 1, RING)])
                    for k in range(RING):
                        s = k % PART
                        pe.wait_ge(s_op, it * RING + (RING + k + 1))
                        with pe.If_ne(mark[k], 0):
                            pe.reg_add(tile, tile, 1)
                            n = pe.snap(tile, min_val=0, max_val=T - 1)
                            pe.wait_ge(s_aggfree, n + 1)
                            pe.reg_mov(at_bank, (n % AGG) * D)
                            pe.matmul(summed(), onehot[:, s, :], hi[:, s, :], start=True, stop=True,
                                      skip_group_check=True)
                        with pe.Else():
                            pe.matmul(summed(), onehot[:, s, :], hi[:, s, :], start=False, stop=True,
                                      skip_group_check=True)
                        pe.matmul(summed(), onehot[:, s, :], lo[:, s, :], start=False, stop=True,
                                  skip_group_check=True).then_inc(s_done, 1)
            pe.wait_ge(s_x1, 1)
            pe.wait_ge(s_fin, 16 * 6)
            pe.wait_ge(s_fb, 16 * 7)
            features, = counters(pe, "features_wanted")
            with pe.Fori(0, GRP) as g:
                pe.wait_ge(s_feat, g + 1)
                for i in range(NT):
                    last = pe.transpose(bank(6)[0:5, i * P:(i + 1) * P], f_in[:, i, :], ident[:, :])
                last.then_inc(s_ftr, 1)
                wait_apart(pe, (s_fte, features, 1))
                for l in range(L - 1):
                    o = 3 * (l % 2)
                    if l:
                        pe.wait_ge(s_ar, g * (L - 1) + l)
                        pe.wait_ge(s_a0, g * (L - 1) + l)
                    for out_rows in (slice(P, G), slice(0, P)):
                        for s in range(2):
                            if l and s and out_rows.start:
                                pe.wait_ge(s_a1, g * (L - 1) + l)
                            r = slice(s * REM, (s + 1) * REM)
                            to = bank(o + 2)[r, :] if out_rows.start else bank(o + s)
                            if l == 0:
                                last = pe.matmul(to, fw_in[:, s, out_rows], feat, start=True, stop=True)
                            else:
                                pe.matmul(to, fwT[:, l - 1, out_rows], act_m[:, (l - 1) % 2, s, :],
                                          start=True, stop=False)
                                last = pe.matmul(to, fwT_r[r, l - 1, out_rows], act_r[r, (l - 1) % 2, :],
                                                 start=False, stop=True)
                            if out_rows.start == 0:
                                last.then_inc((s_p0, s_p1)[s], 1)
                            elif s:
                                last.then_inc(s_pr, 1)
                pe.wait_ge(s_ar, (g + 1) * (L - 1))
                pe.wait_ge(s_a0, (g + 1) * (L - 1))
                pe.wait_ge(s_a1, (g + 1) * (L - 1))
                b = (L - 2) % 2
                for i in range(NT):
                    for s in range(2):
                        to = bank(7 - s)[:, i:i + 1]
                        n = slice(i * P, (i + 1) * P)
                        r = slice(s * REM, (s + 1) * REM)
                        pe.matmul(to, act_m[:, b, s, n], fw_out[:, :], start=True, stop=False)
                        last = pe.matmul(to, act_r[r, b, n], fw_out_r[r, :], start=False, stop=True)
                last.then_inc(s_res, 1)


_INS = ["x", "src", "dst", "edge_weight", "L0_gnn_weight", "L0_ffn_W", "L0_ffn_b"]


def kernel(**inputs):
    import numpy as _np
    import concourse.bacc as _bacc
    from concourse import mybir as _mybir
    from concourse.bass_utils import run_bass_kernel_spmd as _run

    nc = _bacc.Bacc("TRN2", target_bir_lowering=False, num_devices=1)
    arrays, args = {}, []
    for name in _INS:
        a = _np.ascontiguousarray(inputs[name])
        arrays[f"in_{name}"] = a
        args.append(nc.dram_tensor(f"in_{name}", a.shape, _mybir.dt.from_np(a.dtype), kind="ExternalInput").ap())
    args.append(nc.dram_tensor("out_0", inputs["x"].shape, _mybir.dt.float32, kind="ExternalOutput").ap())
    gnn_ffn(nc, *args)
    r = _run(nc, [arrays], core_ids=[0])
    return r.results[0]["out_0"]
```

```python
from contextlib import ExitStack

import concourse.bass as bass
from concourse import mybir

F32 = mybir.dt.float32
F32R = mybir.dt.float32r
I32 = mybir.dt.int32
BF16 = mybir.dt.bfloat16
ALU = mybir.AluOpType
ACT = mybir.ActivationFunctionType
AX_X = mybir.AxisListType.X


def gnn_ffn(nc, x, src, dst, edge_weight, gnn_w, ffn_w, ffn_b, out):
    P = 128
    N, D = x.shape
    E = src.shape[0]
    T = N // P
    COLS = E // P
    CHUNKS = COLS + T
    BLK = 16
    ROWS = CHUNKS * P
    KD = D // P
    REC = 3
    Q = 8
    S_ITERS = COLS // (4 * Q)
    RING = 8
    PART = 4
    AGG = 4
    LOADS = 8
    L, G = ffn_w.shape[0], ffn_w.shape[1]
    GH = G // 2
    LH = L - 2
    NT = 4
    QUARTERS = 4
    QT = T // QUARTERS
    SLOTS = QT * P
    GS = 256
    PASSES = SLOTS // GS
    MARK_AX, OP_MUL, OPVAL = 0, 1, 2 + 27
    IN_A, IN_B, IN_OP, RESULT = 0, 1, 3 + 27, 2
    NIB0, OUT0 = 64, 128
    EPS = 1e-5
    MAGIC = float(3 << 22)
    ZW = 272
    assert CHUNKS % (2 * BLK) == 0 and S_ITERS * 2 == T

    ctx = ExitStack()
    with ctx:
        def sb(name, shape, dt=F32):
            return ctx.enter_context(nc.sbuf_tensor(name, shape, dt))

        def sem(name):
            return ctx.enter_context(nc.semaphore(name))

        h_dram = nc.dram_tensor("h_rows", [N, D], F32, kind="Internal").ap()
        rec_dram = nc.dram_tensor("edge_records", [ROWS, REC], F32, kind="Internal").ap()

        x1 = sb("x1", [P, T, D])
        REGION = 12352
        region = sb("region", [P, REGION])
        at = [0]

        def carve(n, dt=F32):
            at[0] += n
            assert at[0] <= REGION, at[0]
            v = region[:, at[0] - n:at[0]]
            return v if dt == F32 else v.bitcast(dt)

        src_i = carve(COLS, I32)
        dst_i = carve(COLS, I32)
        weight = carve(COLS)
        tile_f = carve(COLS)
        local_i = carve(COLS, I32)
        w_load = carve(KD * D).rearrange("p (k f) -> p k f", k=KD)
        wT = carve(KD * D).rearrange("p (k f) -> p k f", k=KD)
        tail = carve(4 * D)
        xn = tail[:, 0:D]
        xnT = tail[:, D:2 * D].rearrange("p (k n) -> p k n", k=KD)
        h_out = tail[:, 2 * D:4 * D].rearrange("p (s f) -> p s f", s=2)
        junk = tail[:, 0:COLS].bitcast(BF16).rearrange("p (s t) -> p s t", s=2)
        is_first = tail[0:T, 0:CHUNKS]
        iota_c = carve(CHUNKS)[0:T, :]
        src_f = h_out.rearrange("p s f -> p (s f)")
        tile_i = w_load.rearrange("p k f -> p (k f)")[:, 0:COLS].bitcast(I32)
        gathered = region[:, 0:RING * D].rearrange("p (s f) -> p s f", s=RING)
        hi = sb("hi", [P, PART, D], F32R)
        lo = sb("lo", [P, PART, D], F32R)
        onehot = sb("onehot", [P, PART, P], F32R)

        at[0] = 0
        packed = carve(SLOTS + P)[0:5, :]
        answer = carve((SLOTS + P) // 2)[0:1, :].bitcast(BF16)
        slot_hot = carve(2 * NT * P).rearrange("p (b t n) -> p b t n", b=2, t=NT)
        assert at[0] >= RING * D
        fwT = carve(2 * LH * G)[0:GH, :].rearrange("p (h l e) -> p h l e", h=2, l=LH)
        fw_in = carve(2 * G)[0:5, :].rearrange("p (s e) -> p s e", s=2)
        act_f = carve(4 * 2 * GS)[0:GH, :].rearrange("p (b h n) -> p b h n", b=2, h=2)
        fw_load = act_f.rearrange("p b h n -> p (b h n)")[:, 0:2 * LH * G].rearrange("p (h l d) -> p h l d", h=2, l=LH)
        f_res = carve(4 * GS)[0:1, :].rearrange("p (s n) -> p s n", s=2)
        xn_f = carve(NT * P).rearrange("p (t f) -> p t f", t=NT)
        nib = carve(NT * 4 * 16).rearrange("p (t g j) -> p t g j", t=NT, g=4)
        rev16 = carve(NT * 4 * 16).rearrange("p (t g j) -> p t g j", t=NT, g=4)
        hot = carve(NT * 2 * 16).rearrange("p (t s j) -> p t s j", t=NT, s=2)
        marked = carve(T)
        place = carve(T)
        all_sd = carve(T)
        all_rstd = carve(T)
        all_mean = carve(T)
        gain = carve(T)
        shift = carve(T)
        f_in = carve(T * 5).rearrange("p (t c) -> p t c", t=T)
        f_stage = carve(2 * NT * 5).rearrange("p (b t c) -> p b t c", b=2, t=NT)

        squares = region[:, REGION - D:REGION]

        iota_t = sb("iota_t", [P, T])
        iota_p = sb("iota_p", [P, P])
        ident = sb("ident", [P, P])
        before = sb("before", [P, P])
        ones = sb("ones", [P, P])
        zeros = sb("zeros", [P, ZW])
        below = sb("below", [P, T + 1])
        count = sb("count", [P, T])
        counter = sb("counter", [P, 2, T])
        hit = sb("hit", [P, 2, T])
        tot_i = sb("tot_i", [T, 2], I32)
        n_chunks = sb("n_chunks", [T, 2])
        first = sb("first", [T, 1])
        first_diag = sb("first_diag", [T, T])
        flags = sb("flags", [1, CHUNKS + 8], I32)
        rank_f = sb("rank_f", [P, 4 * Q])
        rank_i = sb("rank_i", [P, 4 * Q], I32)
        row_a = sb("row_a", [P, 4 * Q], I32)
        row_b = sb("row_b", [P, 4 * Q], I32)
        row_c = sb("row_c", [P, 4 * Q], I32)
        row = sb("row", [P, 4 * Q], I32)
        rec = sb("rec", [P, 4 * Q, REC])
        stats = sb("stats", [P, 6])
        mv = sb("mv", [P, 2])
        sd = sb("sd", [P, 1])
        rstd = sb("rstd", [P, 1])
        eps = sb("eps", [P, 1])
        meta = sb("meta", [P, 2, BLK, REC])
        all_sum = sb("all_sum", [P, T])
        all_sq = sb("all_sq", [P, T])
        neg_mean = sb("neg_mean", [P, 1])
        f_top = sb("f_top", [P, NT, 4])
        f_val = sb("f_val", [P, NT, 4])
        f_twice = sb("f_twice", [P, NT])
        upto = sb("upto", [1, QT + 1])
        starts = sb("starts", [1, QUARTERS, QT + 4], I32)
        filled = sb("filled", [1, 1])
        active = sb("active", [1, QUARTERS, PASSES], I32)
        zero_row = sb("zero_row", [1, QT])
        f_both = sb("f_both", [P, NT])
        f_both_i = sb("f_both_i", [P, 3, NT], I32)
        f_pair = sb("f_pair", [P, NT, 2])
        ones_b = sb("ones_b", [1, P], BF16)
        bias = sb("bias", [GH, 2, L - 1])
        fw_out = sb("fw_out", [GH, 2])
        b_out = sb("b_out", [1, 1])

        psum = ctx.enter_context(nc.psum_tensor("psum", [P, 8 * D], F32))

        def bank(i, n=1):
            return psum[:, i * D:(i + n) * D]

        s_src, s_dst, s_wt, s_w = sem("src_loaded"), sem("dst_loaded"), sem("weight_loaded"), sem("w_loaded")
        s_x = [sem(f"x_loaded{i}") for i in range(LOADS)]
        s_fill = sem("records_cleared")
        s_const = sem("constants")
        s_v = sem("vector_steps")
        s_cnt = sem("counted")
        s_tot = sem("totals")
        s_nch = sem("chunks_per_tile")
        s_first = sem("first_chunks")
        s_diag = sem("first_diag_ready")
        s_base = sem("group_bases")
        s_isf = sem("is_first_ready")
        s_flagm = sem("flags_summed")
        s_flags = sem("flags_ready")
        s_wtr, s_wev = sem("w_transposed"), sem("w_evacuated")
        s_split = sem("edges_split")
        s_rank = sem("rank_steps")
        s_row = sem("rows_ready")
        s_rec = sem("records_ready")
        s_scat = [sem(f"scattered{q}") for q in range(4)]
        s_var, s_sd, s_xn = sem("variance"), sem("deviation"), sem("normalised")
        s_tr, s_tev, s_mm, s_hev = sem("transposed"), sem("xnT_ready"), sem("multiplied"), sem("h_evacuated")
        s_hst = [sem(f"h_stored{u}") for u in range(2)]
        s_meta = [sem(f"meta_loaded{u}") for u in range(2)]
        s_gat = [sem(f"rows_gathered{k}") for k in range(RING)]
        s_hi = sem("hi_ready")
        s_op = sem("operands_ready")
        s_done = sem("chunks_summed")
        s_aggfree = sem("agg_banks_free")
        s_x1 = sem("x1_ready")

        s_st = sem("ln_steps")
        s_conv = sem("row_steps")
        s_fw, s_fin, s_fb = sem("ffn_w_loaded"), sem("ffn_in_loaded"), sem("ffn_b_loaded")
        s_fz = sem("ffn_in_cleared")
        s_fwt, s_fwe = sem("ffn_w_transposed"), sem("ffn_w_evacuated")
        s_ev = sem("tile_steps")
        s_rev = sem("rev16_and_packed_ready")
        s_gain = sem("gain_and_shift_ready")
        s_alldev = sem("all_deviations")
        s_seq = sem("place_steps")
        s_y = sem("outputs_but_one_hots")
        s_ln = sem("feature_steps")
        s_mark = sem("marks_ready")
        s_rank2 = sem("quarter_ranked")
        s_place = sem("quarter_placed")
        s_hotf = sem("slot_hots_ready")
        s_pk = sem("features_packed_psum")
        s_pke = sem("features_packed")
        s_fs = [sem(f"layer_half{h}_summed") for h in range(2)]
        s_fa = [sem(f"layer_half{h}_ready") for h in range(2)]
        s_res = sem("results_summed")
        s_rese = sem("results_read")
        s_quarter = sem("quarter_answered")
        s_sp = sem("answers_spread")
        s_spe = sem("answers_picked")
        s_hot = sem("one_hots_added")
        s_out = sem("stored")

        block = ctx.enter_context(nc.Block())

        def wait_apart(eng, *waits):
            for _, register, step_by in waits:
                eng.reg_add(register, register, step_by)
            eng.wait_ge(s_const, 7)
            for semaphore, register, _ in waits:
                eng.wait_ge(semaphore, register)

        def counters(eng, *names):
            found = [ctx.enter_context(eng.register(name)) for name in names]
            for register in found:
                eng.reg_mov(register, 0)
            return found

        def at_least(eng, semaphore, value):
            if not (isinstance(value, int) and value == 0):
                eng.wait_ge(semaphore, value)

        @block.sync
        def _(sp):
            sp.dma_start(src_i, src.rearrange("(p t) -> p t", p=P)).then_inc(s_src, 16)
            sp.dma_start(dst_i, dst.rearrange("(p t) -> p t", p=P)).then_inc(s_dst, 16)
            sp.dma_start(weight, edge_weight.rearrange("(p t) -> p t", p=P)).then_inc(s_wt, 16)
            for i in range(LOADS):
                n = T // LOADS
                sp.dma_start(x1[:, i * n:(i + 1) * n, :],
                             x[i * n * P:(i + 1) * n * P, :].rearrange("(t p) f -> p t f", p=P)).then_inc(s_x[i], 16)
            sp.wait_ge(s_const, 7)
            for i in range(ROWS * REC // P // ZW):
                sp.dma_start(rec_dram.rearrange("(p r) c -> p (r c)", p=P)[:, i * ZW:(i + 1) * ZW],
                             zeros[:, :]).then_inc(s_fill, 16)
            sp.wait_ge(s_split, 4)
            sp.dma_start(w_load, gnn_w.rearrange("(k p) f -> p k f", p=P)).then_inc(s_w, 16)
            with sp.Fori(0, S_ITERS) as it:
                for u in range(2):
                    sp.wait_ge(s_hev, it * 2 + (u + 1))
                    sp.dma_start(h_dram[bass.ds((it * 2 + u) * P, P), :], h_out[:, u, :]).then_inc(s_hst[u], 16)
            for q in range(4):
                sp.wait_ge(s_scat[q], 16 * Q * S_ITERS)
            rec_v = rec_dram.rearrange("(b p k) c -> p b (k c)", p=P, k=BLK)
            for u in range(2):
                sp.dma_start(meta[:, u, :, :].rearrange("p k c -> p (k c)"), rec_v[:, u, :]).then_inc(s_meta[u], 16)
            sp.wait_ge(s_fz, 1)
            for h in range(2):
                sp.dma_start(fw_load[:, h, :, :], ffn_w[1:L - 1, h * GH:(h + 1) * GH, :].rearrange("l e d -> e l d")
                             ).then_inc(s_fw, 16)
            with nc.allow_non_contiguous_dma(reason="columns of the first layer, and the biases: a few hundred words"):
                for r, s, c in ((0, 0, IN_A), (2, 0, IN_B), (4, 0, IN_OP), (1, 1, IN_A), (3, 1, IN_B), (4, 1, IN_OP)):
                    sp.dma_start(fw_in[r:r + 1, s, :], ffn_w[0:1, :, c]).then_inc(s_fin, 16)
                for h in range(2):
                    e = slice(h * GH, (h + 1) * GH)
                    sp.dma_start(bias[:, h, :], ffn_b[0:L - 1, e].rearrange("l e -> e l")).then_inc(s_fb, 16)
                    sp.dma_start(fw_out[:, h:h + 1], ffn_w[L - 1, RESULT:RESULT + 1, e].rearrange("a e -> e a")
                                 ).then_inc(s_fb, 16)
                sp.dma_start(b_out[:, :], ffn_b[L - 1:L, RESULT:RESULT + 1]).then_inc(s_fb, 16)
            with sp.Fori(1, CHUNKS // (2 * BLK)) as it:
                for u in range(2):
                    sp.wait_ge(s_op, it * (2 * BLK) + (RING + (u - 1) * BLK))
                    sp.dma_start(meta[:, u, :, :].rearrange("p k c -> p (k c)"),
                                 rec_v[:, bass.ds(it * 2 + u, 1), :]).then_inc(s_meta[u], 16)
            with sp.Fori(0, T // NT) as g:
                sp.wait_ge(s_hot, g + 1)
                sp.dma_start(out[bass.ds(g * (NT * P), NT * P), :].rearrange("(t p) f -> p t f", p=P),
                             x1[:, bass.ds(g * NT, NT), :]).then_inc(s_out, 16)
            sp.wait_ge(s_out, 16 * (T // NT))

        @block.gpsimd
        def _(pool):
            pool.memset(zeros[:, :], 0.0).then_inc(s_const, 1)
            pool.iota(iota_t[:, :], [[1, T]], base=0, channel_multiplier=0,
                      allow_small_or_imprecise_dtypes=True).then_inc(s_const, 1)
            pool.iota(iota_p[:, :], [[1, P]], base=0, channel_multiplier=0,
                      allow_small_or_imprecise_dtypes=True).then_inc(s_const, 1)
            pool.iota(iota_c, [[1, CHUNKS]], base=0, channel_multiplier=0,
                      allow_small_or_imprecise_dtypes=True).then_inc(s_const, 1)
            pool.memset(ones[:, :], 1.0).then_inc(s_const, 1)
            pool.wait_ge(s_const, 5)
            pool.affine_select(out=before[:, :], in_=ones[:, :], compare_op=ALU.is_gt, fill=0.0, base=0,
                               pattern=[[1, P]], channel_multiplier=-1).then_inc(s_const, 1)
            pool.affine_select(out=ident[:, :], in_=ones[:, :], compare_op=ALU.is_equal, fill=0.0, base=0,
                               pattern=[[1, P]], channel_multiplier=-1).then_inc(s_const, 1)
            pool.wait_ge(s_fill, 16 * (ROWS * REC // P // ZW))
            quarters, quarters_too = counters(pool, "rows_wanted", "records_wanted")
            with pool.Fori(0, S_ITERS):
                for q in range(4):
                    wait_apart(pool, (s_row, quarters, 1), (s_rec, quarters_too, 1))
                    for j in range(q * Q, q * Q + Q):
                        pool.indirect_dma_start(rec_dram, bass.IndirectOffsetOnAxis(ap=row[:, j:j + 1], axis=0),
                                                rec[:, j, :], None).then_inc(s_scat[q], 16)
            for u in range(2):
                pool.wait_ge(s_hst[u], 16 * S_ITERS)
            slots, *blocks = counters(pool, "slots_wanted", "even_block_wanted", "odd_block_wanted")
            with pool.Fori(0, CHUNKS // (2 * BLK)):
                for u in range(2):
                    for j in range(BLK):
                        loaded = [(s_meta[u], blocks[u], 16)] if j == 0 else []
                        wait_apart(pool, (s_op, slots, 1), *loaded)
                        pool.indirect_dma_start(
                            gathered[:, j % RING, :], None, h_dram,
                            bass.IndirectOffsetOnAxis(ap=meta[:, u, j, 0:1].bitcast(I32), axis=0),
                        ).then_inc(s_gat[j % RING], 16)

            pool.wait_ge(s_x1, 1)
            pool.memset(packed, 0.0).then_inc(s_rev, 1)
            pool.memset(answer, 0.0).then_inc(s_rev, 1)
            pool.iota(rev16.rearrange("p t g j -> p (t g) j"), [[0, NT * 4], [-1, 16]], base=16, channel_multiplier=0,
                      allow_small_or_imprecise_dtypes=True).then_inc(s_rev, 1)

        @block.scalar
        def _(act):
            act.preload_act_table(ACT.Sqrt)
            for k in range(KD):
                act.wait_ge(s_wtr, k + 1)
                act.activation(wT[:, k, :], bank(k), ACT.Copy).then_inc(s_wev, 1)
            act.wait_ge(s_split, 4)
            act.wait_ge(s_dst, 16)
            act.wait_ge(s_wt, 16)
            def sort_round(it):
                for u in range(2):
                    for q in (2 * u, 2 * u + 1):
                        at_least(act, s_scat[q], it * (16 * Q))
                        c = bass.ds((it * 4 + q) * Q, Q)
                        r = rec[:, q * Q:(q + 1) * Q, :]
                        act.activation(r[:, :, 0].bitcast(I32), dst_i[:, c], ACT.Copy)
                        act.activation(r[:, :, 1], local_i[:, c], ACT.Copy)
                        act.activation(r[:, :, 2], weight[:, c], ACT.Copy).then_inc(s_rec, 1)
                    n = it * 2 + (u + 1)
                    act.wait_ge(s_var, n)
                    act.activation(sd[:, :], mv[:, 1:2], ACT.Sqrt, bias=eps[:, 0:1]).then_inc(s_sd, 1)
                    act.wait_ge(s_tr, n)
                    act.activation(xnT.rearrange("p k n -> p (k n)"), bank(4), ACT.Copy).then_inc(s_tev, 1)
                    act.wait_ge(s_mm, n)
                    at_least(act, s_hst[u], it * 16)
                    act.activation(h_out[:, u, :], bank(5), ACT.Copy).then_inc(s_hev, 1)

            sort_round(0)
            with act.Fori(1, S_ITERS) as it:
                sort_round(it)
            act.wait_ge(s_fwt, 1)
            for l in range(LH):
                act.activation(fwT[:, :, l, :], psum[0:GH, l * D:l * D + 2 * G].rearrange("p (h e) -> p h e", h=2),
                               ACT.Copy).then_inc(s_fwe, 1)
            tile, added, steps, summed = counters(act, "tile", "tiles_added", "stat_steps", "chunks_wanted")
            act.reg_mov(added, AGG)

            def add_tile():
                n = act.snap(tile, min_val=0, max_val=T - 1)
                a = x1[:, bass.ds(n, 1), :].rearrange("p a f -> p (a f)")
                act.activation(a, psum[:, bass.ds((n % AGG) * D, D)], ACT.Copy, accum_out=all_sum[:, bass.ds(n, 1)]
                               ).then_inc(s_aggfree, 1)
                wait_apart(act, (s_aggfree, added, 1))
                act.activation(neg_mean[:, :], all_sum[:, bass.ds(n, 1)], ACT.Copy, scale=-1.0 / D).then_inc(s_ev, 1)
                wait_apart(act, (s_ev, steps, 1))
                act.activation(squares, a, ACT.Square, bias=neg_mean[:, 0:1], accum_out=all_sq[:, bass.ds(n, 1)]
                               ).then_inc(s_ev, 1)
                act.reg_add(steps, steps, 1)
                act.reg_add(tile, tile, 1)

            mark = [ctx.enter_context(act.register(f"amark{k}")) for k in range(RING)]
            with act.Fori(0, CHUNKS // RING) as it:
                act.reg_load(mark, flags[0:1, bass.ds(it * RING, RING)])
                for k in range(RING):
                    b = (it // 2) % 2
                    w = meta[:, bass.ds(b, 1), bass.ds((it % 2) * RING + k, 1), 2]
                    act.wait_ge(s_gat[k], it * 16 + 16)
                    act.wait_ge(s_done, it * RING + (k + 1))
                    act.activation(hi[:, k % PART, :], gathered[:, k, :], ACT.Copy,
                                   scale=w.rearrange("p a b -> p (a b)")).then_inc(s_hi, 1)
                    with act.If_ne(mark[k], 0):
                        act.reg_mov(summed, it * RING + (k + PART - 2))
                        wait_apart(act, (s_done, summed, 1))
                        add_tile()
            act.reg_load(mark[0], flags[0:1, CHUNKS:CHUNKS + 1])
            act.wait_ge(s_done, CHUNKS + PART)
            with act.If_ne(mark[0], 0):
                add_tile()
            add_tile()
            act.wait_ge(s_ev, 2 * T)
            act.activation(all_sd[:, :], all_sq[:, :], ACT.Sqrt, bias=eps[:, 0:1], scale=1.0 / D).then_inc(s_alldev, 1)
            act.wait_ge(s_fb, 16 * 5)
            act.wait_ge(s_rev, 3)
            base = [ctx.enter_context(act.register(f"abase{i}")) for i in range(NT)]
            layers, go = counters(act, "layers_wanted", "act_pass_active")

            def pack_tiles(h, g):
                act.reg_load(base, starts[0:1, h, bass.ds(g * NT, NT)])
                act.wait_ge(s_pk, g + (h * (QT // NT) + 3))
                for i in range(NT):
                    b = act.snap(base[i], min_val=0, max_val=SLOTS)
                    at_least(act, s_pke, g * NT + (h * QT + i))
                    act.activation(packed[:, bass.ds(b, P)], bank(5)[0:5, i * P:(i + 1) * P], ACT.Copy
                                   ).then_inc(s_pke, 1)

            def layers_of_pass(tiles):
                each = -(-len(tiles) // (L - 1))
                for l in range(L - 1):
                    act.reg_add(layers, layers, 1)
                    for e in range(2):
                        act.wait_ge(s_fs[e], layers)
                        act.activation(act_f[:, l % 2, e, :], bank(2 * (l % 2) + e)[0:GH, :], ACT.Relu,
                                       bias=bias[:, e, l:l + 1]).then_inc(s_fa[e], 1)
                    for n in tiles[l * each:(l + 1) * each]:
                        act.activation(x1[:, n, :], x1[:, n, :], ACT.Identity, bias=shift[:, n:n + 1],
                                       scale=gain[:, n:n + 1]).then_inc(s_y, 1)

            for h in range(QUARTERS):
                act.wait_ge(s_place, h + 1)
                pack_tiles(h, 0)
                with act.Fori(1, QT // NT) as g:
                    pack_tiles(h, g)
                act.wait_ge(s_mark, (h + 1) * (QT // NT))
                act.wait_ge(s_gain, 2)
                layers_of_pass(range(h * QT, (h + 1) * QT))
                with act.Fori(1, PASSES) as g:
                    act.reg_load(go, active[0:1, h, bass.ds(g, 1)])
                    with act.If_ne(go, 0):
                        layers_of_pass([])

        @block.vector
        def _(dve):
            steps = [0]

            def step(ins):
                steps[0] += 1
                ins.then_inc(s_v, 1)
                dve.wait_ge(s_v, steps[0])

            dve.memset(eps[:, :], EPS)
            dve.memset(below[:, 0:1], 0.0)
            dve.memset(below[:, T:T + 1], float(COLS))
            step(dve.memset(flags[:, :], 0))
            dve.wait_ge(s_src, 16)
            dve.tensor_copy(src_f, src_i).then_inc(s_split, 1)
            dve.tensor_scalar(tile_i, src_i, 7, None, ALU.arith_shift_right).then_inc(s_split, 1)
            dve.tensor_scalar(local_i, src_i, P - 1, None, ALU.bitwise_and).then_inc(s_split, 1)
            dve.wait_ge(s_split, 2)
            dve.tensor_copy(tile_f, tile_i).then_inc(s_split, 1)
            for b in range(1, T):
                if b >= 3:
                    dve.wait_ge(s_cnt, b - 2)
                dve.tensor_scalar(junk[:, b % 2, :], src_f, float(b * P), None, ALU.is_lt, ALU.add,
                                  accum_out=below[:, b:b + 1]).then_inc(s_cnt, 1)
            dve.wait_ge(s_cnt, T - 1)
            dve.tensor_tensor(count[:, :], below[:, 1:T + 1], below[:, 0:T], ALU.subtract).then_inc(s_cnt, 1)
            dve.wait_ge(s_tot, 1)
            step(dve.tensor_scalar(tot_i[:, 0:1], bank(6)[0:T, 0:1], float(P - 1), None, ALU.add))
            step(dve.tensor_scalar(tot_i[:, 1:2], tot_i[:, 0:1], 7, None, ALU.arith_shift_right))
            dve.tensor_scalar(n_chunks[:, 0:1], tot_i[:, 1:2], 1.0, None, ALU.max).then_inc(s_nch, 1)
            dve.wait_ge(s_first, 1)
            step(dve.tensor_copy(first[:, :], bank(6)[0:T, 64:65]))
            dve.tensor_scalar(first_diag[:, :], ident[0:T, 0:T], first[:, 0:1], float(P),
                              ALU.mult, ALU.mult).then_inc(s_diag, 1)
            dve.tensor_scalar(is_first, iota_c, first[:, 0:1], None, ALU.is_equal).then_inc(s_isf, 1)
            dve.wait_ge(s_base, 1)
            step(dve.tensor_copy(counter[:, 0, :], bank(7)[:, 0:T]))
            dve.wait_ge(s_flagm, 1)
            dve.tensor_copy(flags[:, 2:CHUNKS + 1], psum[0:1, 1:CHUNKS]).then_inc(s_flags, 1)
            dve.wait_ge(s_flags, 1)
            dve.wait_ge(s_split, 4)
            for i in range(LOADS):
                dve.wait_ge(s_x[i], 16)

            ln_wanted, = counters(dve, "ln_steps_wanted")
            def sort_round(it):
                for u in range(2):
                    for q in (2 * u, 2 * u + 1):
                        for j in range(Q):
                            a, b = j % 2, 1 - j % 2
                            t = tile_f[:, bass.ds(it * (4 * Q) + (q * Q + j), 1)]
                            at_least(dve, s_rank, it * (8 * Q) + 2 * (q * Q + j))
                            dve.scalar_tensor_tensor(hit[:, a, :], iota_t[:, :], t, counter[:, a, :], ALU.is_equal,
                                                     ALU.mult, accum_out=rank_f[:, q * Q + j:q * Q + j + 1]
                                                     ).then_inc(s_rank, 1)
                            dve.scalar_tensor_tensor(counter[:, b, :], iota_t[:, :], t, counter[:, a, :],
                                                     ALU.is_equal, ALU.add).then_inc(s_rank, 1)
                        s = slice(q * Q, (q + 1) * Q)
                        dve.wait_ge(s_rank, it * (8 * Q) + 2 * (q + 1) * Q)
                        base = (it * 4 + q) * 5
                        dve.tensor_copy(rank_i[:, s], rank_f[:, s]).then_inc(s_conv, 1)
                        dve.wait_ge(s_conv, base + 1)
                        dve.tensor_scalar(row_a[:, s], rank_i[:, s], P - 1, 4, ALU.bitwise_and,
                                          ALU.logical_shift_left).then_inc(s_conv, 1)
                        dve.tensor_scalar(row_b[:, s], rank_i[:, s], 7, BLK - 1, ALU.arith_shift_right,
                                          ALU.bitwise_and).then_inc(s_conv, 1)
                        dve.tensor_scalar(row_c[:, s], rank_i[:, s], ~(BLK * P - 1), None,
                                          ALU.bitwise_and).then_inc(s_conv, 1)
                        dve.wait_ge(s_conv, base + 4)
                        dve.tensor_tensor(row_a[:, s], row_a[:, s], row_b[:, s], ALU.bitwise_or).then_inc(s_conv, 1)
                        dve.wait_ge(s_conv, base + 5)
                        at_least(dve, s_scat[q], it * (16 * Q))
                        dve.tensor_tensor(row[:, s], row_a[:, s], row_c[:, s], ALU.bitwise_or).then_inc(s_row, 1)
                    n = it * 2 + u
                    dve.bn_stats(stats[:, :], x1[:, bass.ds(n, 1), :].rearrange("p a f -> p (a f)")).then_inc(s_st, 1)
                    dve.reg_mov(ln_wanted, n * 2)
                    wait_apart(dve, (s_st, ln_wanted, 1))
                    dve.bn_aggr(mv[:, :], stats[:, :]).then_inc(s_var, 1)
                    dve.wait_ge(s_sd, n + 1)
                    dve.reciprocal(rstd[:, :], sd[:, :]).then_inc(s_st, 1)
                    dve.wait_ge(s_st, n * 2 + 2)
                    at_least(dve, s_tr, n)
                    dve.tensor_scalar(xn, x1[:, bass.ds(n, 1), :].rearrange("p a f -> p (a f)"), mv[:, 0:1],
                                      rstd[:, 0:1], ALU.subtract, ALU.mult).then_inc(s_xn, 1)
                    dve.wait_ge(s_xn, n + 1)

            sort_round(0)
            with dve.Fori(1, S_ITERS) as it:
                sort_round(it)

            dve.wait_ge(s_tr, T)
            dve.wait_ge(s_tev, T)
            dve.memset(hit[:, 0, 0:1], 0.0).then_inc(s_op, RING)
            dve.memset(hit[:, 1, 0:1], 0.0).then_inc(s_aggfree, AGG)
            dve.wait_ge(s_hst[0], 16 * S_ITERS)
            dve.wait_ge(s_hst[1], 16 * S_ITERS)
            dve.memset(fw_in, 0.0).then_inc(s_fz, 1)

            with dve.Fori(0, CHUNKS // RING) as it:
                for k in range(RING):
                    c = it * RING + k
                    b, j = (it // 2) % 2, (it % 2) * RING + k
                    m = meta[:, bass.ds(b, 1), bass.ds(j, 1), :].rearrange("p a b c -> p (a b c)")
                    dve.wait_ge(s_hi, c + 1)
                    dve.wait_ge(s_done, c + 1)
                    dve.scalar_tensor_tensor(lo[:, k % PART, :], gathered[:, k, :], m[:, 2:3],
                                             hi[:, k % PART, :].bitcast(F32), ALU.mult, ALU.subtract)
                    dve.tensor_scalar(onehot[:, k % PART, :], iota_p[:, :], m[:, 1:2], None,
                                      ALU.is_equal).then_inc(s_op, 1)
            dve.wait_ge(s_ev, 2 * T)
            dve.memset(zero_row[:, :], 0.0).then_inc(s_pk, 2)
            dve.memset(upto[:, :], 0.0).then_inc(s_rese, 1)
            dve.memset(f_both[:, :], 0.0).then_inc(s_spe, 1)
            dve.memset(ones_b[:, :], 1.0).then_inc(s_x1, 1)
            dve.wait_ge(s_x1, 1)

            seq = [0]

            def done(ins):
                seq[0] += 1
                ins.then_inc(s_seq, 1)
                dve.wait_ge(s_seq, seq[0])

            dve.wait_ge(s_alldev, 1)
            dve.tensor_scalar(all_mean[:, :], all_sum[:, :], 1.0 / D, None, ALU.mult)
            dve.reciprocal(all_rstd[:, :], all_sd[:, :]).then_inc(s_ev, 1)
            dve.wait_ge(s_ev, 2 * T + 1)
            dve.tensor_scalar(gain[:, :], all_rstd[:, :], 1.0, None, ALU.add).then_inc(s_gain, 1)
            dve.scalar_tensor_tensor(shift[:, :], all_mean[:, :], -1.0, all_rstd[:, :], ALU.mult, ALU.mult
                                     ).then_inc(s_gain, 1)
            dve.wait_ge(s_rev, 3)
            feature_steps, = counters(dve, "feature_steps_wanted")

            def again(ins):
                ins.then_inc(s_ln, 1)
                dve.reg_add(feature_steps, feature_steps, 1)
                dve.wait_ge(s_ln, feature_steps)

            def find_features(h):
                with dve.Fori(h * (QT // NT), (h + 1) * (QT // NT)) as g:
                    for i in range(NT):
                        n = bass.ds(g * NT + i, 1)
                        last = dve.tensor_scalar(xn_f[:, i, :], x1[:, n, 0:P].rearrange("p a f -> p (a f)"),
                                                 all_mean[:, n], all_rstd[:, n], ALU.subtract, ALU.mult)
                    again(last)
                    again(dve.scalar_tensor_tensor(nib.rearrange("p t g j -> p t (g j)"), xn_f[:, :, NIB0:NIB0 + 64], 0.5,
                                                   rev16.rearrange("p t g j -> p t (g j)"), ALU.is_gt, ALU.mult))
                    again(dve.tensor_reduce(f_top[:, :, :], nib, AX_X, ALU.max))
                    dve.tensor_scalar(f_twice[:, :], xn_f[:, :, MARK_AX], 0.5, None, ALU.is_ge)
                    again(dve.tensor_scalar(f_val[:, :, :], f_top[:, :, :], -1.0, 16.0, ALU.mult, ALU.add))
                    t = bass.ds(g * NT, NT)
                    dve.tensor_copy(f_in[:, t, 4:5], xn_f[:, :, OPVAL:OPVAL + 1])
                    dve.scalar_tensor_tensor(f_in[:, t, 0:4], f_top[:, :, :], 0.0, f_val[:, :, :], ALU.is_gt, ALU.mult)
                    dve.scalar_tensor_tensor(marked[:, t], xn_f[:, :, OP_MUL], 0.5, f_twice[:, :],
                                             ALU.is_ge, ALU.mult).then_inc(s_mark, 1)
                    dve.wait_ge(s_mark, g + 1)

            def place_quarter(h):
                t = slice(h * QT, (h + 1) * QT)
                dve.wait_ge(s_rank2, h + 1)
                done(dve.scalar_tensor_tensor(place[:, t], bank(7)[:, 0:QT], 1.0, marked[:, t], ALU.add, ALU.mult))
                done(dve.tensor_scalar(place[:, t], place[:, t], -1.0, None, ALU.add))
                done(dve.tensor_tensor_scan(upto[:, 1:QT + 1], bank(7)[0:1, QT:2 * QT], zero_row[:, :], 0.0, ALU.add, ALU.add))
                done(dve.tensor_copy(starts[:, h, 0:QT + 1], upto[:, :]))
                done(dve.tensor_scalar(filled[:, :], upto[:, QT:QT + 1], 1.0 / GS, 0.5, ALU.mult, ALU.max))
                dve.tensor_scalar(active[:, h, :], iota_p[0:1, 0:PASSES], filled[:, 0:1], None, ALU.is_lt
                                  ).then_inc(s_place, 1)
                dve.wait_ge(s_place, h + 1)

            def slot_hots(h):
                with dve.Fori(0, QT // NT // 2) as g2:
                    for b in range(2):
                        g = g2 * 2 + b
                        t = bass.ds(g * NT + h * QT, NT)
                        dve.wait_ge(s_pk, g + (h * (QT // NT) + 1))
                        dve.tensor_copy(f_stage[:, b, :, :], f_in[:, t, :])
                        dve.tensor_tensor(slot_hot[:, b, :, :], iota_p[:, :].unsqueeze(1).to_broadcast([P, NT, P]),
                                          place[:, t].unsqueeze(2).to_broadcast([P, NT, P]), ALU.is_equal
                                          ).then_inc(s_hotf, 1)

            pass_no, go = counters(dve, "results_wanted", "dve_pass_active")

            def answers(h):
                dve.wait_ge(s_rev, 3)
                with dve.Fori(0, PASSES) as g:
                    dve.reg_load(go, active[0:1, h, bass.ds(g, 1)])
                    with dve.If_ne(go, 0):
                        dve.reg_add(pass_no, pass_no, 1)
                        dve.wait_ge(s_res, pass_no)
                        again(dve.tensor_scalar(f_res[:, 0, :], bank(4)[0:1, :], b_out[:, 0:1], MAGIC, ALU.add, ALU.add))
                        again(dve.tensor_scalar(f_res[:, 1, :], f_res[:, 0, :], MAGIC, 0.0, ALU.subtract, ALU.max))
                        again(dve.tensor_scalar(f_res[:, 0, :], f_res[:, 1, :], 15.0, None, ALU.min))
                        again(dve.scalar_tensor_tensor(answer[:, bass.ds(g * GS, GS)], f_res[:, 0, GS:2 * GS], 16.0,
                                                       f_res[:, 0, 0:GS], ALU.mult, ALU.add))
                        dve.memset(f_res[:, 1, 0:1], 0.0).then_inc(s_rese, 1)
                dve.memset(f_res[:, 1, 1:2], 0.0).then_inc(s_quarter, 1)

            def add_hots(h):
                with dve.Fori(0, QT // NT) as g:
                    t = bass.ds(g * NT + h * QT, NT)
                    dve.wait_ge(s_sp, g + (h * (QT // NT) + 1))
                    for i in range(NT):
                        p = place[:, bass.ds(g * NT + (h * QT + i), 1)]
                        last = dve.scalar_tensor_tensor(slot_hot[:, 0, i, :], iota_p[:, :], p,
                                                        bank(6)[:, i * P:(i + 1) * P], ALU.is_equal, ALU.mult,
                                                        accum_out=f_both[:, i:i + 1])
                    last.then_inc(s_spe, 1)
                    dve.wait_ge(s_spe, g + (h * (QT // NT) + 2))
                    again(dve.tensor_copy(f_both_i[:, 0, :], f_both[:, :]))
                    dve.tensor_scalar(f_both_i[:, 1, :], f_both_i[:, 0, :], 15, None, ALU.bitwise_and)
                    dve.tensor_scalar(f_twice[:, :], marked[:, t], 2.0, None, ALU.mult)
                    again(dve.tensor_scalar(f_both_i[:, 2, :], f_both_i[:, 0, :], 4, None, ALU.arith_shift_right))
                    again(dve.tensor_copy(f_pair.rearrange("p t s -> p s t"), f_both_i[:, 1:3, :]))
                    again(dve.tensor_tensor(hot.rearrange("p t s j -> p (t s) j"),
                                            iota_p[:, 0:16].unsqueeze(1).to_broadcast([P, 2 * NT, 16]),
                                            f_pair.rearrange("p t s -> p (t s)").unsqueeze(2).to_broadcast([P, 2 * NT, 16]),
                                            ALU.is_equal))
                    again(dve.tensor_tensor(hot.rearrange("p t s j -> p t (s j)"), hot.rearrange("p t s j -> p t (s j)"),
                                            f_twice[:, :].unsqueeze(2).to_broadcast([P, NT, 32]), ALU.mult))
                    dve.wait_ge(s_y, g * NT + (h * QT + NT))
                    dve.tensor_tensor(x1[:, t, OUT0:OUT0 + 32], x1[:, t, OUT0:OUT0 + 32],
                                      hot.rearrange("p t s j -> p t (s j)"), ALU.add).then_inc(s_hot, 1)
                    dve.wait_ge(s_hot, g + (h * (QT // NT) + 1))

            find_features(0)
            place_quarter(0)
            slot_hots(0)
            for h in range(QUARTERS):
                if h + 1 < QUARTERS:
                    find_features(h + 1)
                answers(h)
                if h + 1 < QUARTERS:
                    place_quarter(h + 1)
                    slot_hots(h + 1)
                add_hots(h)

        @block.tensor
        def _(pe):
            pe.wait_ge(s_const, 7)
            pe.wait_ge(s_w, 16)
            for k in range(KD):
                for j in range(KD):
                    last = pe.transpose(bank(k)[:, j * P:(j + 1) * P], w_load[:, j, k * P:(k + 1) * P], ident[:, :])
                last.then_inc(s_wtr, 1)
            pe.wait_ge(s_cnt, T)
            pe.matmul(bank(6)[0:T, 0:1], count[:, :], ones[:, 0:1], start=True, stop=True).then_inc(s_tot, 1)
            pe.wait_ge(s_nch, 1)
            pe.matmul(bank(6)[0:T, 64:65], before[0:T, 0:T], n_chunks[:, 0:1], start=True, stop=True).then_inc(s_first, 1)
            pe.wait_ge(s_diag, 1)
            pe.matmul(bank(7)[:, 0:T], before[:, :], count[:, :], start=True, stop=False)
            pe.matmul(bank(7)[:, 0:T], ones[0:T, :], first_diag[:, :], start=False, stop=True).then_inc(s_base, 1)
            pe.wait_ge(s_isf, 1)
            pe.wait_ge(s_wev, KD)
            for c in range(0, CHUNKS, D):
                e = min(CHUNKS, c + D)
                last = pe.matmul(psum[0:1, c:e], ones[0:T, 0:1], is_first[:, c:e], start=True, stop=True)
            last.then_inc(s_flagm, 1)
            with pe.Fori(0, T) as n:
                pe.wait_ge(s_xn, n + 1)
                for k in range(KD):
                    last = pe.transpose(bank(4)[:, k * P:(k + 1) * P], xn[:, k * P:(k + 1) * P], ident[:, :])
                last.then_inc(s_tr, 1)
                pe.wait_ge(s_tev, n + 1)
                for k in range(KD):
                    last = pe.matmul(bank(5), xnT[:, k, :], wT[:, k, :], start=(k == 0), stop=(k == KD - 1))
                last.then_inc(s_mm, 1)
            pe.wait_ge(s_flags, 1)
            pe.wait_ge(s_hev, T)
            pe.wait_ge(s_fw, 32)
            for l in range(LH):
                for d in range(2):
                    for e in range(2):
                        o = l * D + d * G + e * GH
                        last = pe.transpose(psum[0:GH, o:o + GH], fw_load[:, e, l, d * GH:(d + 1) * GH],
                                            ident[0:GH, 0:GH])
            last.then_inc(s_fwt, 1)
            pe.wait_ge(s_fwe, LH)
            pe.matmul(bank(0), ident[:, :], x1[:, 0, :], start=True, stop=False, skip_group_check=True
                      ).then_inc(s_done, PART)
            with ExitStack() as regs:
                mark = [regs.enter_context(pe.register(f"pmark{k}")) for k in range(RING)]
                tile = regs.enter_context(pe.register("ptile"))
                at_bank = regs.enter_context(pe.register("pbank"))
                pe.reg_mov(tile, 0)
                pe.reg_mov(at_bank, 0)

                def summed():
                    return psum[:, bass.ds(pe.snap(at_bank, min_val=0, max_val=(AGG - 1) * D), D)]

                with pe.Fori(0, CHUNKS // RING) as it:
                    pe.reg_load(mark, flags[0:1, bass.ds(it * RING + 1, RING)])
                    for k in range(RING):
                        s = k % PART
                        pe.wait_ge(s_op, it * RING + (RING + k + 1))
                        with pe.If_ne(mark[k], 0):
                            pe.reg_add(tile, tile, 1)
                            n = pe.snap(tile, min_val=0, max_val=T - 1)
                            pe.wait_ge(s_aggfree, n + 1)
                            pe.reg_mov(at_bank, (n % AGG) * D)
                            pe.matmul(summed(), ident[:, :], x1[:, bass.ds(n, 1), :].rearrange("p a f -> p (a f)"),
                                      start=True, stop=False, skip_group_check=True)
                        pe.matmul(summed(), onehot[:, s, :], hi[:, s, :], start=False, stop=True,
                                  skip_group_check=True)
                        pe.matmul(summed(), onehot[:, s, :], lo[:, s, :], start=False, stop=True,
                                  skip_group_check=True).then_inc(s_done, 1)
            pe.wait_ge(s_x1, 1)
            pe.wait_ge(s_fin, 16 * 6)
            pe.wait_ge(s_fb, 16 * 5)
            base = [ctx.enter_context(pe.register(f"pbase{i}")) for i in range(NT)]
            layers, pass_no, packs, go = counters(pe, "layers_done", "passes_done", "packs_wanted", "pe_pass_active")

            def rank_quarter(h):
                t = slice(h * QT, (h + 1) * QT)
                pe.wait_ge(s_mark, (h + 1) * (QT // NT))
                if h:
                    pe.wait_ge(s_place, h)
                pe.matmul(bank(7)[:, 0:QT], before[:, :], marked[:, t], start=True, stop=True)
                pe.matmul(bank(7)[:, QT:2 * QT], ones[:, :], marked[:, t], start=True, stop=True).then_inc(s_rank2, 1)

            def pack_quarter(h):
                with pe.Fori(0, QT // NT // 2) as g2:
                    for b in range(2):
                        g = g2 * 2 + b
                        wait_apart(pe, (s_hotf, packs, 1))
                        for i in range(NT):
                            last = pe.matmul(bank(5)[0:5, i * P:(i + 1) * P], f_stage[:, b, i, :], slot_hot[:, b, i, :],
                                             start=True, stop=True)
                        last.then_inc(s_pk, 1)
                        pe.wait_ge(s_pke, g * NT + (h * QT + NT))

            def layers_quarter(h):
                with pe.Fori(0, PASSES) as g:
                    pe.reg_load(go, active[0:1, h, bass.ds(g, 1)])
                    with pe.If_ne(go, 0):
                        for l in range(L - 1):
                            if l:
                                pe.reg_add(layers, layers, 1)
                            for e in range(2):
                                to = bank(2 * (l % 2) + e)[0:GH, :]
                                rows = slice(e * GH, (e + 1) * GH)
                                if l == 0:
                                    for s in range(2):
                                        last = pe.matmul(to[:, s * GS:(s + 1) * GS], fw_in[:, s, rows],
                                                         packed[:, bass.ds(g * GS, GS)], start=True, stop=True)
                                else:
                                    for d in range(2):
                                        if e == 0:
                                            pe.wait_ge(s_fa[d], layers)
                                        last = pe.matmul(to, fwT[:, d, l - 1, rows], act_f[:, (l - 1) % 2, d, :],
                                                         start=(d == 0), stop=(d == 1))
                                last.then_inc(s_fs[e], 1)
                        pe.reg_add(layers, layers, 1)
                        pe.reg_add(pass_no, pass_no, 1)
                        for d in range(2):
                            pe.wait_ge(s_fa[d], layers)
                        pe.wait_ge(s_rese, pass_no)
                        for d in range(2):
                            last = pe.matmul(bank(4)[0:1, :], fw_out[:, d:d + 1], act_f[:, (L - 2) % 2, d, :],
                                             start=(d == 0), stop=(d == 1))
                        last.then_inc(s_res, 1)

            def spread_quarter(h):
                pe.wait_ge(s_quarter, h + 1)
                with pe.Fori(0, QT // NT) as g:
                    pe.reg_load(base, starts[0:1, h, bass.ds(g * NT, NT)])
                    pe.wait_ge(s_spe, g + (h * (QT // NT) + 1))
                    for i in range(NT):
                        b = pe.snap(base[i], min_val=0, max_val=SLOTS)
                        last = pe.matmul(bank(6)[:, i * P:(i + 1) * P], ones_b[:, :], answer[:, bass.ds(b, P)],
                                         start=True, stop=True)
                    last.then_inc(s_sp, 1)

            rank_quarter(0)
            pack_quarter(0)
            for h in range(QUARTERS):
                layers_quarter(h)
                if h + 1 < QUARTERS:
                    rank_quarter(h + 1)
                    pack_quarter(h + 1)
                spread_quarter(h)


_INS = ["x", "src", "dst", "edge_weight", "L0_gnn_weight", "L0_ffn_W", "L0_ffn_b"]


def kernel(**inputs):
    import numpy as _np
    import concourse.bacc as _bacc
    from concourse import mybir as _mybir
    from concourse.bass_utils import run_bass_kernel_spmd as _run

    nc = _bacc.Bacc("TRN2", target_bir_lowering=False, num_devices=1)
    arrays, args = {}, []
    for name in _INS:
        a = _np.ascontiguousarray(inputs[name])
        arrays[f"in_{name}"] = a
        args.append(nc.dram_tensor(f"in_{name}", a.shape, _mybir.dt.from_np(a.dtype), kind="ExternalInput").ap())
    args.append(nc.dram_tensor("out_0", inputs["x"].shape, _mybir.dt.float32, kind="ExternalOutput").ap())
    gnn_ffn(nc, *args)
    r = _run(nc, [arrays], core_ids=[0])
    return r.results[0]["out_0"]
```

```python
from contextlib import ExitStack

import concourse.bass as bass
from concourse import mybir

F32 = mybir.dt.float32
F32R = mybir.dt.float32r
I32 = mybir.dt.int32
BF16 = mybir.dt.bfloat16
ALU = mybir.AluOpType
ACT = mybir.ActivationFunctionType
AX_X = mybir.AxisListType.X


def gnn_ffn(nc, x, src, dst, edge_weight, gnn_w, ffn_w, ffn_b, out):
    P = 128
    N, D = x.shape
    E = src.shape[0]
    T = N // P
    COLS = E // P
    CHUNKS = COLS + T
    SPLIT = 42
    BLK = 16
    ROWS = CHUNKS * P
    KD = D // P
    REC = 3
    Q = 8
    S_ITERS = COLS // (4 * Q)
    RING = 8
    ROUNDS = CHUNKS // RING
    R = 2 * BLK // RING
    PART = 4
    LAG = PART - 1
    AGG = 4
    LOADS = 8
    L, G = ffn_w.shape[0], ffn_w.shape[1]
    GH = G // 2
    GP = 96
    LH = L - 2
    NT = 4
    QUARTERS = 4
    QT = T // QUARTERS
    SLOTS = QT * P
    GROUPS = QT // NT
    NH = 8
    FIRST_PACK = 2
    GS = 216
    PASSES = -(-SLOTS // GS)
    MARK_AX, OP_MUL, OPVAL = 0, 1, 2 + 27
    IN_A, IN_B, IN_OP, RESULT = 0, 1, 3 + 27, 2
    NIB0, OUT0 = 64, 128
    EPS = 1e-5
    MAGIC = float(3 << 22)
    ZW = 136
    assert CHUNKS % (2 * BLK) == 0 and COLS % (2 * BLK) == 0 and S_ITERS * 2 == T

    ctx = ExitStack()
    with ctx:
        def sb(name, shape, dt=F32):
            return ctx.enter_context(nc.sbuf_tensor(name, shape, dt))

        def sem(name):
            return ctx.enter_context(nc.semaphore(name))

        h_dram = nc.dram_tensor("h_rows", [N, D], F32, kind="Internal").ap()
        rec_dram = nc.dram_tensor("edge_records", [ROWS, REC], F32, kind="Internal").ap()

        x1 = sb("x1", [P, T, D])
        REGION = 12352
        region = sb("region", [P, REGION])
        at = [0]

        def carve(n, dt=F32):
            at[0] += n
            assert at[0] <= REGION, at[0]
            v = region[:, at[0] - n:at[0]]
            return v if dt == F32 else v.bitcast(dt)

        src_i = carve(COLS, I32)
        dst_i = carve(COLS, I32)
        weight = carve(COLS)
        tile_f = carve(COLS)
        local_i = carve(COLS, I32)
        w_load = carve(KD * D).rearrange("p (k f) -> p k f", k=KD)
        wT = carve(KD * D).rearrange("p (k f) -> p k f", k=KD)
        tail = carve(4 * D)
        xn = tail[:, 0:D]
        xnT = tail[:, D:2 * D].rearrange("p (k n) -> p k n", k=KD)
        h_out = tail[:, 2 * D:4 * D].rearrange("p (s f) -> p s f", s=2)
        junk = tail[:, 0:COLS].bitcast(BF16).rearrange("p (s t) -> p s t", s=2)
        junk_a = wT.rearrange("p k f -> p (k f)")[:, 0:COLS].bitcast(BF16).rearrange("p (s t) -> p s t", s=2)
        is_first = tail[0:T, 0:CHUNKS]
        iota_c = carve(CHUNKS)[0:T, :]
        tile_b = h_out.rearrange("p s f -> p (s f)")[:, 0:COLS // 2].bitcast(BF16)
        tile_i = w_load.rearrange("p k f -> p (k f)")[:, 0:COLS].bitcast(I32)
        gathered = region[:, 0:RING * D].rearrange("p (s f) -> p s f", s=RING)
        hi = sb("hi", [P, PART, D], F32R)
        lo = sb("lo", [P, PART, D], F32R)
        onehot = sb("onehot", [P, PART, P], F32R)

        at[0] = 0
        slot_hot = carve(QT * P).rearrange("p (t n) -> p t n", t=QT)
        nib = carve(QT * 64).rearrange("p (t j) -> p t j", t=QT)
        hot = carve(NH * 2 * 16).rearrange("p (t s j) -> p t s j", t=NH, s=2)
        f_twice = carve(NH)
        f_both = carve(NH)
        f_both_i = carve(3 * NH, I32).rearrange("p (s t) -> p s t", s=3)
        f_pair = carve(2 * NH).rearrange("p (t s) -> p t s", t=NH)
        picks = carve(3 * QT).rearrange("p (t c) -> p t c", t=QT)
        mark_axis = carve(QT).rearrange("p (t c) -> p t c", t=QT)
        f_top = carve(QT * 4).rearrange("p (t g) -> p t g", t=QT)
        f_val = carve(QT * 4).rearrange("p (t g) -> p t g", t=QT)
        marked = carve(T)
        place = carve(T)
        all_sd = carve(T)
        all_rstd = carve(T)
        all_mean = carve(T)
        gain = carve(T)
        shift = carve(T)
        f_in = carve(T * 5).rearrange("p (t c) -> p t c", t=T)
        assert at[0] >= RING * D
        wide = max(SLOTS + P, PASSES * GS)
        both = carve(wide)
        packed = both[0:GP, :]
        f_res = both[GP:GP + 1, 0:4 * GS].rearrange("p (s n) -> p s n", s=2)
        answer = carve(wide // 2)[0:1, :].bitcast(BF16)
        all_fwT = carve(2 * LH * 2 * GP)[0:GP, :]
        fwT = all_fwT.rearrange("p (h l e) -> p h l e", h=2, l=LH)
        all_fw_in = carve(4 * GP)[0:GP, :]
        fw_in = all_fw_in.rearrange("p (s e) -> p s e", s=2)
        act_f = carve(4 * 2 * GS)[0:GP, :].rearrange("p (b h n) -> p b h n", b=2, h=2)
        fw_load = act_f.rearrange("p b h n -> p (b h n)")[0:GH, 0:2 * LH * G].rearrange("p (h l d) -> p h l d", h=2, l=LH)
        junk_b = carve(D // 2).bitcast(BF16)

        iota_t = sb("iota_t", [P, T])
        iota_p = sb("iota_p", [P, P])
        ident = sb("ident", [P, P])
        before = sb("before", [P, P])
        ones = sb("ones", [P, P])
        zeros = sb("zeros", [P, ZW])
        below = sb("below", [P, T + 1])
        count = sb("count", [P, T])
        counter = sb("counter", [P, 2, T])
        hit = sb("hit", [P, 2, T])
        tot_i = sb("tot_i", [T, 2], I32)
        n_chunks = sb("n_chunks", [T, 2])
        first = sb("first", [T, 1])
        first_diag = sb("first_diag", [T, T])
        flags = sb("flags", [1, CHUNKS + 8], I32)
        live = sb("live", [1, ROUNDS], I32)
        live_to = sb("live_to", [1, 1])
        rank_f = sb("rank_f", [P, 4 * Q])
        rank_i = sb("rank_i", [P, 4 * Q], I32)
        row_a = sb("row_a", [P, 4 * Q], I32)
        row_b = sb("row_b", [P, 4 * Q], I32)
        row_c = sb("row_c", [P, 4 * Q], I32)
        row = sb("row", [P, 4 * Q], I32)
        rec = sb("rec", [P, 4 * Q, REC])
        stats = sb("stats", [P, 6])
        mv = sb("mv", [P, 2])
        sd = sb("sd", [P, 1])
        rstd = sb("rstd", [P, 1])
        eps = sb("eps", [P, 1])
        meta = sb("meta", [P, 2, BLK, REC])
        all_sum = sb("all_sum", [P, T])
        all_sq = sb("all_sq", [P, T])
        threshold, sign_sum = all_sum, all_sq
        neg_mean = sb("neg_mean", [P, 1])
        upto = sb("upto", [1, QT + 1])
        rev = sb("rev", [P, 64])
        starts = sb("starts", [1, QUARTERS, QT + 4], I32)
        alone = sb("alone", [1, QUARTERS], I32)
        filled = sb("filled", [1, 1])
        active = sb("active", [1, QUARTERS, PASSES], I32)
        zero_row = sb("zero_row", [1, QT])
        ones_b = sb("ones_b", [1, P], BF16)
        bias = sb("bias", [GP, 2, L - 1])
        fw_out = sb("fw_out", [GP, 2])
        b_out = sb("b_out", [1, 1])

        psum = ctx.enter_context(nc.psum_tensor("psum", [P, 8 * D], F32))

        def bank(i, n=1):
            return psum[:, i * D:(i + n) * D]

        s_src, s_dst, s_wt, s_w = sem("src_loaded"), sem("dst_loaded"), sem("weight_loaded"), sem("w_loaded")
        s_x = [sem(f"x_loaded{i}") for i in range(LOADS)]
        s_fill = sem("records_cleared")
        s_const = sem("constants")
        s_v = sem("vector_steps")
        s_cnt = sem("counted")
        s_tot = sem("totals")
        s_nch = sem("chunks_per_tile")
        s_first = sem("first_chunks")
        s_diag = sem("first_diag_ready")
        s_base = sem("group_bases")
        s_thr, s_sign = sem("thresholds_ready"), sem("signs_summed")
        s_isf = sem("is_first_ready")
        s_flagm = sem("flags_summed")
        s_flags = sem("flags_ready")
        s_wtr, s_wev = sem("w_transposed"), sem("w_evacuated")
        s_split = sem("edges_split")
        s_rank = sem("rank_steps")
        s_row = sem("rows_ready")
        s_rec = sem("records_ready")
        s_scat = [sem(f"scattered{q}") for q in range(4)]
        s_var, s_sd, s_xn = sem("variance"), sem("deviation"), sem("normalised")
        s_tr, s_tev, s_mm, s_hev = sem("transposed"), sem("xnT_ready"), sem("multiplied"), sem("h_evacuated")
        s_hst = [sem(f"h_stored{u}") for u in range(2)]
        s_meta = [sem(f"meta_loaded{u}") for u in range(2)]
        s_gat = [sem(f"rows_gathered{k}") for k in range(RING)]
        s_hi = sem("hi_ready")
        s_op = sem("operands_ready")
        s_done = sem("chunks_summed")
        s_aggfree = sem("agg_banks_free")
        s_x1 = sem("x1_ready")

        s_st = sem("ln_steps")
        s_conv = sem("row_steps")
        s_fw, s_fin, s_fb = sem("ffn_w_loaded"), sem("ffn_in_loaded"), sem("ffn_b_loaded")
        s_fz = sem("ffn_in_cleared")
        s_fwt, s_fwe = sem("ffn_w_transposed"), sem("ffn_w_evacuated")
        s_ev = sem("tile_steps")
        s_norm = sem("normalise_steps")
        s_gain = sem("gain_and_shift_ready")
        s_alldev = sem("all_deviations")
        s_seq = sem("place_steps")
        s_y = sem("outputs_but_one_hots")
        s_ln = sem("feature_steps")
        s_mark = sem("marks_ready")
        s_rank2 = sem("quarter_ranked")
        s_place = sem("quarter_placed")
        s_hotf = sem("slot_hots_ready")
        s_pk = sem("features_packed_psum")
        s_pke = sem("features_packed")
        s_fs = [sem(f"layer_half{h}_summed") for h in range(2)]
        s_fa = [sem(f"layer_half{h}_ready") for h in range(2)]
        s_res = sem("results_summed")
        s_rese = sem("results_read")
        s_quarter = sem("quarter_answered")
        s_sp = sem("answers_spread")
        s_spe = sem("answers_picked")
        s_hot = sem("one_hots_added")
        s_out = sem("stored")

        block = ctx.enter_context(nc.Block())

        def wait_apart(eng, *waits):
            for _, register, step_by in waits:
                eng.reg_add(register, register, step_by)
            eng.wait_ge(s_const, 8)
            for semaphore, register, _ in waits:
                eng.wait_ge(semaphore, register)

        def rounds(eng, go, one_round):
            with eng.Fori(0, COLS // (2 * BLK)) as it:
                for r in range(R):
                    one_round(it, r, it * (2 * BLK) + r * RING)
            with eng.Fori(COLS // (2 * BLK), CHUNKS // (2 * BLK)) as it:
                for r in range(R):
                    eng.reg_load(go, live[0:1, bass.ds(it * R + r, 1)])
                    with eng.If_ne(go, 0):
                        one_round(it, r, it * (2 * BLK) + r * RING)

        def counters(eng, *names):
            found = [ctx.enter_context(eng.register(name)) for name in names]
            for register in found:
                eng.reg_mov(register, 0)
            return found

        def at_least(eng, semaphore, value):
            if not (isinstance(value, int) and value == 0):
                eng.wait_ge(semaphore, value)

        def normalise(eng, h):
            t = slice(h * QT, (h + 1) * QT)

            def wide(a, n):
                return a[:, t].unsqueeze(2).to_broadcast([P, QT, n])

            eng.tensor_tensor(nib, x1[:, t, NIB0:NIB0 + 64], wide(all_mean, 64), ALU.subtract)
            eng.tensor_tensor(picks[:, :, 0:2], x1[:, t, MARK_AX:MARK_AX + 2], wide(all_mean, 2), ALU.subtract)
            eng.tensor_tensor(picks[:, :, 2:3], x1[:, t, OPVAL:OPVAL + 1], wide(all_mean, 1), ALU.subtract
                              ).then_inc(s_norm, 1)
            eng.wait_ge(s_norm, 2 * h + 1)
            eng.tensor_tensor(picks, picks, wide(all_rstd, 3), ALU.mult)
            eng.tensor_tensor(nib, nib, wide(all_rstd, 64), ALU.mult).then_inc(s_norm, 1)

        @block.sync
        def _(sp):
            sp.dma_start(src_i, src.rearrange("(p t) -> p t", p=P)).then_inc(s_src, 16)
            sp.dma_start(dst_i, dst.rearrange("(p t) -> p t", p=P)).then_inc(s_dst, 16)
            sp.dma_start(weight, edge_weight.rearrange("(p t) -> p t", p=P)).then_inc(s_wt, 16)
            for i in range(LOADS):
                if i == 2:
                    sp.wait_ge(s_const, 8)
                    for j in range(ROWS * REC // P // ZW):
                        sp.dma_start(rec_dram.rearrange("(p r) c -> p (r c)", p=P)[:, j * ZW:(j + 1) * ZW],
                                     zeros[:, :]).then_inc(s_fill, 16)
                    sp.wait_ge(s_split, 4)
                    sp.dma_start(w_load, gnn_w.rearrange("(k p) f -> p k f", p=P)).then_inc(s_w, 16)
                n = T // LOADS
                sp.dma_start(x1[:, i * n:(i + 1) * n, :],
                             x[i * n * P:(i + 1) * n * P, :].rearrange("(t p) f -> p t f", p=P)).then_inc(s_x[i], 16)
            with sp.Fori(0, S_ITERS) as it:
                for u in range(2):
                    sp.wait_ge(s_hev, it * 2 + (u + 1))
                    sp.dma_start(h_dram[bass.ds((it * 2 + u) * P, P), :], h_out[:, u, :]).then_inc(s_hst[u], 16)
            for q in range(4):
                sp.wait_ge(s_scat[q], 16 * Q * S_ITERS)
            rec_v = rec_dram.rearrange("(b p k) c -> p b (k c)", p=P, k=BLK)
            for u in range(2):
                sp.dma_start(meta[:, u, :, :].rearrange("p k c -> p (k c)"), rec_v[:, u, :]).then_inc(s_meta[u], 16)
            sp.wait_ge(s_fz, 6)
            for h in range(2):
                sp.dma_start(fw_load[:, h, :, :], ffn_w[1:L - 1, h * GH:(h + 1) * GH, :].rearrange("l e d -> e l d")
                             ).then_inc(s_fw, 16)
            with nc.allow_non_contiguous_dma(reason="columns of the first layer, and the biases: a few hundred words"):
                for r, s, c in ((0, 0, IN_A), (2, 0, IN_B), (4, 0, IN_OP), (1, 1, IN_A), (3, 1, IN_B), (4, 1, IN_OP)):
                    for h in range(2):
                        sp.dma_start(fw_in[r:r + 1, s, h * GP:h * GP + GH], ffn_w[0:1, h * GH:(h + 1) * GH, c]
                                     ).then_inc(s_fin, 16)
                for h in range(2):
                    e = slice(h * GH, (h + 1) * GH)
                    sp.dma_start(bias[0:GH, h, :], ffn_b[0:L - 1, e].rearrange("l e -> e l")).then_inc(s_fb, 16)
                    sp.dma_start(fw_out[0:GH, h:h + 1], ffn_w[L - 1, RESULT:RESULT + 1, e].rearrange("a e -> e a")
                                 ).then_inc(s_fb, 16)
                sp.dma_start(b_out[:, :], ffn_b[L - 1:L, RESULT:RESULT + 1]).then_inc(s_fb, 16)
            sp.wait_ge(s_flags, 1)
            go, = counters(sp, "sp_block_live")

            def load_block(it, u):
                sp.wait_ge(s_op, it * (2 * BLK) + (RING + (u - 1) * BLK))
                sp.dma_start(meta[:, u, :, :].rearrange("p k c -> p (k c)"),
                             rec_v[:, bass.ds(it * 2 + u, 1), :]).then_inc(s_meta[u], 16)

            with sp.Fori(1, COLS // (2 * BLK)) as it:
                for u in range(2):
                    load_block(it, u)
            with sp.Fori(COLS // (2 * BLK), CHUNKS // (2 * BLK)) as it:
                for u in range(2):
                    sp.reg_load(go, live[0:1, bass.ds(it * (2 * BLK // RING) + u * (BLK // RING), 1)])
                    with sp.If_ne(go, 0):
                        load_block(it, u)
            out_v = out.rearrange("(t p) f -> p t f", p=P)
            late = OUT0 + 32

            def store_hots(h):
                for k in range(h * (QT // NH), (h + 1) * (QT // NH)):
                    t = slice(k * NH, (k + 1) * NH)
                    sp.wait_ge(s_hot, k + 1)
                    sp.dma_start(out_v[:, t, 0:late], x1[:, t, 0:late]).then_inc(s_out, 16)

            for h in range(QUARTERS):
                t = slice(h * QT, (h + 1) * QT)
                sp.wait_ge(s_y, (h + 1) * QT)
                sp.dma_start(out_v[:, t, late:D], x1[:, t, late:D]).then_inc(s_out, 16)
                if h:
                    store_hots(h - 1)
            store_hots(QUARTERS - 1)
            sp.wait_ge(s_out, 16 * (QUARTERS + T // NH))

        @block.gpsimd
        def _(pool):
            pool.memset(zeros[:, :], 0.0).then_inc(s_const, 1)
            pool.iota(iota_t[:, :], [[1, T]], base=0, channel_multiplier=0,
                      allow_small_or_imprecise_dtypes=True).then_inc(s_const, 1)
            pool.iota(iota_p[:, :], [[1, P]], base=0, channel_multiplier=0,
                      allow_small_or_imprecise_dtypes=True).then_inc(s_const, 1)
            pool.iota(iota_c, [[1, CHUNKS]], base=0, channel_multiplier=0,
                      allow_small_or_imprecise_dtypes=True).then_inc(s_const, 1)
            pool.iota(rev[:, :], [[0, 4], [-1, 16]], base=16, channel_multiplier=0,
                      allow_small_or_imprecise_dtypes=True).then_inc(s_const, 1)
            pool.memset(ones[:, :], 1.0).then_inc(s_const, 1)
            pool.wait_ge(s_const, 6)
            pool.affine_select(out=before[:, :], in_=ones[:, :], compare_op=ALU.is_gt, fill=0.0, base=0,
                               pattern=[[1, P]], channel_multiplier=-1).then_inc(s_const, 1)
            pool.affine_select(out=ident[:, :], in_=ones[:, :], compare_op=ALU.is_equal, fill=0.0, base=0,
                               pattern=[[1, P]], channel_multiplier=-1).then_inc(s_const, 1)
            pool.wait_ge(s_fill, 16 * (ROWS * REC // P // ZW))
            quarters, quarters_too = counters(pool, "rows_wanted", "records_wanted")
            with pool.Fori(0, S_ITERS):
                for q in range(4):
                    wait_apart(pool, (s_row, quarters, 1), (s_rec, quarters_too, 1))
                    for j in range(q * Q, q * Q + Q):
                        pool.indirect_dma_start(rec_dram, bass.IndirectOffsetOnAxis(ap=row[:, j:j + 1], axis=0),
                                                rec[:, j, :], None).then_inc(s_scat[q], 16)
            for u in range(2):
                pool.wait_ge(s_hst[u], 16 * S_ITERS)
            pool.wait_ge(s_flags, 1)
            go, slots, *blocks = counters(pool, "pool_round_live", "slots_wanted", "even_block_wanted", "odd_block_wanted")

            def gather(u, r):
                for k in range(RING):
                    loaded = [(s_meta[u], blocks[u], 16)] if r == 0 and k == 0 else []
                    wait_apart(pool, (s_op, slots, 1), *loaded)
                    pool.indirect_dma_start(
                        gathered[:, k, :], None, h_dram,
                        bass.IndirectOffsetOnAxis(ap=meta[:, u, r * RING + k, 0:1].bitcast(I32), axis=0),
                    ).then_inc(s_gat[k], 16)

            with pool.Fori(0, COLS // (2 * BLK)):
                for u in range(2):
                    for r in range(BLK // RING):
                        gather(u, r)
            with pool.Fori(COLS // (2 * BLK), CHUNKS // (2 * BLK)) as it:
                for u in range(2):
                    for r in range(BLK // RING):
                        pool.reg_load(go, live[0:1, bass.ds(it * (2 * BLK // RING) + (u * (BLK // RING) + r), 1)])
                        with pool.If_ne(go, 0):
                            gather(u, r)

            for h in range(QUARTERS):
                pool.wait_ge(s_mark, h + 1)
                if h + 1 < QUARTERS:
                    normalise(pool, h + 1)
                for n in range(h * QT, (h + 1) * QT):
                    pool.tensor_scalar(x1[:, n, :], x1[:, n, :], gain[:, n:n + 1], shift[:, n:n + 1],
                                       ALU.mult, ALU.add).then_inc(s_y, 1)

        @block.scalar
        def _(act):
            act.preload_act_table(ACT.Sign)
            act.wait_ge(s_split, 4)
            act.wait_ge(s_thr, 1)
            for b in range(SPLIT, T):
                if b >= SPLIT + 2:
                    act.wait_ge(s_sign, b - SPLIT - 1)
                act.activation(junk_a[:, b % 2, :], tile_f, ACT.Sign, bias=threshold[:, b:b + 1],
                               accum_out=sign_sum[:, b:b + 1]).then_inc(s_sign, 1)
            act.wait_ge(s_sign, T - SPLIT)
            act.preload_act_table(ACT.Sqrt)
            act.wait_ge(s_split, 4)
            act.wait_ge(s_dst, 16)
            act.wait_ge(s_wt, 16)
            def sort_round(it):
                for u in range(2):
                    for q in (2 * u, 2 * u + 1):
                        at_least(act, s_scat[q], it * (16 * Q))
                        c = bass.ds((it * 4 + q) * Q, Q)
                        r = rec[:, q * Q:(q + 1) * Q, :]
                        act.activation(r[:, :, 0].bitcast(I32), dst_i[:, c], ACT.Copy)
                        act.activation(r[:, :, 1], local_i[:, c], ACT.Copy)
                        act.activation(r[:, :, 2], weight[:, c], ACT.Copy).then_inc(s_rec, 1)
                    if isinstance(it, int) and u == 0:
                        for k in range(KD):
                            act.wait_ge(s_wtr, k + 1)
                            act.activation(wT[:, k, :], bank(k), ACT.Copy).then_inc(s_wev, 1)
                    n = it * 2 + (u + 1)
                    act.wait_ge(s_var, n)
                    act.activation(sd[:, :], mv[:, 1:2], ACT.Sqrt, bias=eps[:, 0:1]).then_inc(s_sd, 1)
                    act.wait_ge(s_tr, n)
                    act.activation(xnT.rearrange("p k n -> p (k n)"), bank(4), ACT.Copy).then_inc(s_tev, 1)
                    act.wait_ge(s_mm, n)
                    at_least(act, s_hst[u], it * 16)
                    act.activation(h_out[:, u, :], bank(5), ACT.Copy).then_inc(s_hev, 1)

            sort_round(0)
            with act.Fori(1, S_ITERS) as it:
                sort_round(it)
            go, tile, added, steps, summed = counters(act, "act_live", "tile", "tiles_added", "stat_steps", "all_summed")
            act.reg_mov(summed, PART)
            act.reg_mov(added, AGG)

            def add_tile():
                n = act.snap(tile, min_val=0, max_val=T - 1)
                a = x1[:, bass.ds(n, 1), :].rearrange("p a f -> p (a f)")
                act.activation(a, psum[:, bass.ds((n % AGG) * D, D)], ACT.Copy, accum_out=all_sum[:, bass.ds(n, 1)]
                               ).then_inc(s_aggfree, 1)
                wait_apart(act, (s_aggfree, added, 1))
                act.activation(neg_mean[:, :], all_sum[:, bass.ds(n, 1)], ACT.Copy, scale=-1.0 / D).then_inc(s_ev, 1)
                wait_apart(act, (s_ev, steps, 1))
                act.activation(junk_b, a, ACT.Square, bias=neg_mean[:, 0:1], accum_out=all_sq[:, bass.ds(n, 1)]
                               ).then_inc(s_ev, 1)
                act.reg_add(steps, steps, 1)
                act.reg_add(tile, tile, 1)

            mark = [ctx.enter_context(act.register(f"amark{k}")) for k in range(RING)]
            def one_round(it, r, c):
                act.reg_add(summed, summed, RING)
                act.reg_load(mark, flags[0:1, bass.ds(c, RING)])
                for k in range(RING):
                    act.wait_ge(s_gat[k], it * (16 * R) + 16 * (r + 1))
                    act.wait_ge(s_done, c + (k + 1))
                    act.activation(hi[:, k % PART, :], gathered[:, k, :], ACT.Copy,
                                   scale=meta[:, r * RING // BLK, r * RING % BLK + k, 2:3]).then_inc(s_hi, 1)
                    with act.If_ne(mark[k], 0):
                        add_tile()
            rounds(act, go, one_round)
            act.reg_load(mark[0:LAG], flags[0:1, CHUNKS:CHUNKS + LAG])
            act.wait_ge(s_const, 8)
            act.wait_ge(s_done, summed)
            for k in range(LAG):
                with act.If_ne(mark[k], 0):
                    add_tile()
            add_tile()
            act.wait_ge(s_ev, 2 * T)
            act.activation(all_sd[:, :], all_sq[:, :], ACT.Sqrt, bias=eps[:, 0:1], scale=1.0 / D).then_inc(s_alldev, 1)
            act.wait_ge(s_fwt, 1)
            for l in range(LH):
                for h in range(2):
                    last = act.activation(fwT[0:GH, h, l, :].rearrange("p (s e) -> p s e", s=2)[:, :, 0:GH],
                                          psum[0:GH, l * D + h * G:l * D + (h + 1) * G].rearrange("p (s e) -> p s e", s=2),
                                          ACT.Copy)
                last.then_inc(s_fwe, 1)
            act.wait_ge(s_fb, 16 * 5)
            base = [ctx.enter_context(act.register(f"abase{i}")) for i in range(NT)]
            layers, single = counters(act, "layers_wanted", "act_alone")

            def pack_tiles(h, g):
                act.wait_ge(s_place, h + 1)
                act.reg_load(base, starts[0:1, h, g * NT:(g + 1) * NT])
                act.wait_ge(s_pk, h * GROUPS + g + 1)
                for i in range(NT):
                    b = act.snap(base[i], min_val=0, max_val=SLOTS)
                    at_least(act, s_pke, h * QT + g * NT + i)
                    act.activation(packed[0:5, bass.ds(b, P)], bank(5 + 2 * (g % 2))[0:5, i * P:(i + 1) * P], ACT.Copy
                                   ).then_inc(s_pke, 1)

            def layers_of_pass(between):
                for l in range(L - 1):
                    act.reg_add(layers, layers, 1)
                    for e in range(2):
                        act.wait_ge(s_fs[e], layers)
                        act.activation(act_f[:, l % 2, e, :], bank(2 * (l % 2) + e)[0:GP, 0:2 * GS], ACT.Relu,
                                       bias=bias[:, e, l:l + 1]).then_inc(s_fa[e], 1)
                    if l in between:
                        with act.If_ne(single, 0):
                            pack_tiles(*between[l])

            for g in range(GROUPS):
                pack_tiles(0, g)
            for h in range(QUARTERS):
                act.wait_ge(s_place, h + 1)
                act.reg_load(single, alone[0:1, h:h + 1])
                layers_of_pass({FIRST_PACK + g: (h + 1, g) for g in range(GROUPS)} if h + 1 < QUARTERS else {})
                act.reg_load(go, active[0:1, h, 1:2])
                with act.If_ne(go, 0):
                    with act.Fori(1, PASSES) as g:
                        act.reg_load(go, active[0:1, h, bass.ds(g, 1)])
                        with act.If_ne(go, 0):
                            layers_of_pass({})
                    if h + 1 < QUARTERS:
                        for g in range(GROUPS):
                            pack_tiles(h + 1, g)

        @block.vector
        def _(dve):
            steps = [0]

            def step(ins):
                steps[0] += 1
                ins.then_inc(s_v, 1)
                dve.wait_ge(s_v, steps[0])

            dve.memset(eps[:, :], EPS)
            dve.memset(below[:, 0:1], 0.0)
            dve.memset(below[:, T:T + 1], float(COLS))
            step(dve.memset(flags[:, :], 0))
            dve.wait_ge(s_src, 16)
            dve.tensor_scalar(tile_i, src_i, 7, None, ALU.arith_shift_right).then_inc(s_split, 1)
            dve.wait_ge(s_split, 1)
            dve.tensor_copy(tile_f, tile_i).then_inc(s_split, 1)
            dve.tensor_copy(tile_b, tile_i).then_inc(s_split, 1)
            dve.tensor_scalar(local_i, src_i, P - 1, None, ALU.bitwise_and).then_inc(s_split, 1)
            dve.wait_ge(s_const, 8)
            dve.tensor_scalar(threshold[:, :], iota_t[:, :], -1.0, 0.5, ALU.mult, ALU.add).then_inc(s_thr, 1)
            dve.wait_ge(s_split, 4)
            for b in range(1, SPLIT):
                if b >= 3:
                    dve.wait_ge(s_cnt, b - 2)
                dve.tensor_scalar(junk[:, b % 2, :], tile_b, float(b), None, ALU.is_lt, ALU.add,
                                  accum_out=below[:, b:b + 1]).then_inc(s_cnt, 1)
            dve.wait_ge(s_sign, T - SPLIT)
            dve.tensor_scalar(below[:, SPLIT:T], sign_sum[:, SPLIT:T], -0.5, COLS / 2, ALU.mult, ALU.add).then_inc(s_cnt, 1)
            dve.wait_ge(s_cnt, SPLIT)
            dve.tensor_tensor(count[:, :], below[:, 1:T + 1], below[:, 0:T], ALU.subtract).then_inc(s_cnt, 1)
            dve.wait_ge(s_tot, 1)
            step(dve.tensor_scalar(tot_i[:, 0:1], bank(6)[0:T, 0:1], float(P - 1), None, ALU.add))
            step(dve.tensor_scalar(tot_i[:, 1:2], tot_i[:, 0:1], 7, None, ALU.arith_shift_right))
            dve.tensor_scalar(n_chunks[:, 0:1], tot_i[:, 1:2], 1.0, None, ALU.max).then_inc(s_nch, 1)
            dve.wait_ge(s_first, 1)
            step(dve.tensor_scalar(live_to[:, :], bank(6)[0:1, 128:129], float(LAG), None, ALU.add))
            dve.tensor_scalar(live[:, :], iota_c[0:1, 0:ROUNDS], float(RING), live_to[:, 0:1], ALU.mult, ALU.is_lt)
            step(dve.tensor_copy(first[:, :], bank(6)[0:T, 64:65]))
            dve.tensor_scalar(first_diag[:, :], ident[0:T, 0:T], first[:, 0:1], float(P),
                              ALU.mult, ALU.mult).then_inc(s_diag, 1)
            dve.tensor_scalar(is_first, iota_c, first[:, 0:1], None, ALU.is_equal).then_inc(s_isf, 1)
            dve.wait_ge(s_base, 1)
            step(dve.tensor_copy(counter[:, 0, :], bank(7)[:, 0:T]))
            dve.wait_ge(s_split, 4)

            ln_wanted, = counters(dve, "ln_steps_wanted")
            def sort_round(it):
                for u in range(2):
                    for q in (2 * u, 2 * u + 1):
                        for j in range(Q):
                            a, b = j % 2, 1 - j % 2
                            t = tile_f[:, bass.ds(it * (4 * Q) + (q * Q + j), 1)]
                            at_least(dve, s_rank, it * (8 * Q) + 2 * (q * Q + j))
                            dve.scalar_tensor_tensor(hit[:, a, :], iota_t[:, :], t, counter[:, a, :], ALU.is_equal,
                                                     ALU.mult, accum_out=rank_f[:, q * Q + j:q * Q + j + 1]
                                                     ).then_inc(s_rank, 1)
                            dve.scalar_tensor_tensor(counter[:, b, :], iota_t[:, :], t, counter[:, a, :],
                                                     ALU.is_equal, ALU.add).then_inc(s_rank, 1)
                        s = slice(q * Q, (q + 1) * Q)
                        dve.wait_ge(s_rank, it * (8 * Q) + 2 * (q + 1) * Q)
                        base = (it * 4 + q) * 5
                        dve.tensor_copy(rank_i[:, s], rank_f[:, s]).then_inc(s_conv, 1)
                        dve.wait_ge(s_conv, base + 1)
                        dve.tensor_scalar(row_a[:, s], rank_i[:, s], P - 1, 4, ALU.bitwise_and,
                                          ALU.logical_shift_left).then_inc(s_conv, 1)
                        dve.tensor_scalar(row_b[:, s], rank_i[:, s], 7, BLK - 1, ALU.arith_shift_right,
                                          ALU.bitwise_and).then_inc(s_conv, 1)
                        dve.tensor_scalar(row_c[:, s], rank_i[:, s], ~(BLK * P - 1), None,
                                          ALU.bitwise_and).then_inc(s_conv, 1)
                        dve.wait_ge(s_conv, base + 4)
                        dve.tensor_tensor(row_a[:, s], row_a[:, s], row_b[:, s], ALU.bitwise_or).then_inc(s_conv, 1)
                        dve.wait_ge(s_conv, base + 5)
                        at_least(dve, s_scat[q], it * (16 * Q))
                        dve.tensor_tensor(row[:, s], row_a[:, s], row_c[:, s], ALU.bitwise_or).then_inc(s_row, 1)
                    n = it * 2 + u
                    if isinstance(it, int) and u == 0:
                        dve.wait_ge(s_flagm, 1)
                        dve.tensor_copy(flags[:, LAG + 1:CHUNKS + LAG], psum[0:1, 1:CHUNKS]).then_inc(s_flags, 1)
                        dve.wait_ge(s_flags, 1)
                        dve.wait_ge(s_x[0], 16)
                    dve.bn_stats(stats[:, :], x1[:, bass.ds(n, 1), :].rearrange("p a f -> p (a f)")).then_inc(s_st, 1)
                    dve.reg_mov(ln_wanted, n * 2)
                    wait_apart(dve, (s_st, ln_wanted, 1))
                    dve.bn_aggr(mv[:, :], stats[:, :]).then_inc(s_var, 1)
                    dve.wait_ge(s_sd, n + 1)
                    dve.reciprocal(rstd[:, :], sd[:, :]).then_inc(s_st, 1)
                    dve.wait_ge(s_st, n * 2 + 2)
                    at_least(dve, s_tr, n)
                    dve.tensor_scalar(xn, x1[:, bass.ds(n, 1), :].rearrange("p a f -> p (a f)"), mv[:, 0:1],
                                      rstd[:, 0:1], ALU.subtract, ALU.mult).then_inc(s_xn, 1)
                    dve.wait_ge(s_xn, n + 1)

            sort_round(0)
            for i in range(1, LOADS):
                dve.wait_ge(s_x[i], 16)
            with dve.Fori(1, S_ITERS) as it:
                sort_round(it)

            dve.wait_ge(s_tr, T)
            dve.wait_ge(s_tev, T)
            dve.memset(hit[:, 0, 0:1], 0.0).then_inc(s_op, RING)
            dve.memset(hit[:, 1, 0:1], 0.0).then_inc(s_aggfree, AGG)
            dve.wait_ge(s_hst[0], 16 * S_ITERS)
            dve.wait_ge(s_hst[1], 16 * S_ITERS)
            for cleared in (packed, answer, all_fwT, all_fw_in, bias.rearrange("p h l -> p (h l)"), fw_out[:, :]):
                dve.memset(cleared, 0.0).then_inc(s_fz, 1)

            go, = counters(dve, "dve_live")
            def one_round(it, r, c):
                for k in range(RING):
                    m = meta[:, r * RING // BLK, r * RING % BLK + k, :]
                    dve.wait_ge(s_hi, c + (k + 1))
                    dve.wait_ge(s_done, c + (k + 1))
                    dve.scalar_tensor_tensor(lo[:, k % PART, :], gathered[:, k, :], m[:, 2:3],
                                             hi[:, k % PART, :].bitcast(F32), ALU.mult, ALU.subtract)
                    dve.tensor_scalar(onehot[:, k % PART, :], iota_p[:, :], m[:, 1:2], None,
                                      ALU.is_equal).then_inc(s_op, 1)
            rounds(dve, go, one_round)
            dve.wait_ge(s_ev, 2 * T)
            dve.memset(zero_row[:, :], 0.0)
            dve.memset(upto[:, :], 0.0).then_inc(s_rese, 1)
            dve.memset(ones_b[:, :], 1.0).then_inc(s_x1, 1)
            dve.wait_ge(s_x1, 1)

            seq = [0]

            def done(ins):
                seq[0] += 1
                ins.then_inc(s_seq, 1)
                dve.wait_ge(s_seq, seq[0])

            dve.wait_ge(s_alldev, 1)
            dve.tensor_scalar(all_mean[:, :], all_sum[:, :], 1.0 / D, None, ALU.mult)
            dve.reciprocal(all_rstd[:, :], all_sd[:, :]).then_inc(s_ev, 1)
            dve.wait_ge(s_ev, 2 * T + 1)
            dve.tensor_scalar(gain[:, :], all_rstd[:, :], 1.0, None, ALU.add).then_inc(s_gain, 1)
            dve.scalar_tensor_tensor(shift[:, :], all_mean[:, :], -1.0, all_rstd[:, :], ALU.mult, ALU.mult
                                     ).then_inc(s_gain, 1)
            dve.wait_ge(s_gain, 2)
            feature_steps, = counters(dve, "feature_steps_wanted")

            def again(ins):
                ins.then_inc(s_ln, 1)
                dve.reg_add(feature_steps, feature_steps, 1)
                dve.wait_ge(s_ln, feature_steps)

            def find_features(h):
                t = slice(h * QT, (h + 1) * QT)
                dve.wait_ge(s_norm, 2 * h + 2)
                dve.tensor_scalar(mark_axis, picks[:, :, 0:1], 0.5, None, ALU.is_ge)
                done(dve.scalar_tensor_tensor(nib, nib, 0.5, rev[:, :].unsqueeze(1).to_broadcast([P, QT, 64]),
                                              ALU.is_gt, ALU.mult))
                dve.scalar_tensor_tensor(marked[:, t].unsqueeze(2), picks[:, :, 1:2], 0.5, mark_axis, ALU.is_ge, ALU.mult)
                dve.tensor_copy(f_in[:, t, 4:5], picks[:, :, 2:3])
                done(dve.tensor_reduce(f_top, nib.rearrange("p t (g j) -> p t g j", g=4), AX_X, ALU.max))
                done(dve.tensor_scalar(f_val, f_top, -1.0, 16.0, ALU.mult, ALU.add))
                dve.scalar_tensor_tensor(f_in[:, t, 0:4], f_top, 0.0, f_val, ALU.is_gt, ALU.mult).then_inc(s_mark, 1)
                dve.wait_ge(s_mark, h + 1)

            def place_quarter(h):
                t = slice(h * QT, (h + 1) * QT)
                dve.wait_ge(s_rank2, h + 1)
                done(dve.scalar_tensor_tensor(place[:, t], bank(7)[:, 0:QT], 1.0, marked[:, t], ALU.add, ALU.mult))
                done(dve.tensor_scalar(place[:, t], place[:, t], -1.0, None, ALU.add))
                done(dve.tensor_tensor_scan(upto[:, 1:QT + 1], bank(7)[0:1, QT:2 * QT], zero_row[:, :], 0.0, ALU.add, ALU.add))
                done(dve.tensor_copy(starts[:, h, 0:QT + 1], upto[:, :]))
                done(dve.tensor_scalar(filled[:, :], upto[:, QT:QT + 1], 1.0 / GS, None, ALU.mult))
                dve.tensor_scalar(alone[:, h:h + 1], filled[:, :], 1.0, None, ALU.is_le)
                dve.tensor_scalar(active[:, h, :], iota_p[0:1, 0:PASSES], filled[:, 0:1], None, ALU.is_lt
                                  ).then_inc(s_place, 1)
                dve.wait_ge(s_place, h + 1)

            def slot_hots(h):
                at_least(dve, s_pk, h * GROUPS)
                for g in range(GROUPS):
                    t = slice(h * QT + g * NT, h * QT + (g + 1) * NT)
                    dve.tensor_tensor(slot_hot[:, g * NT:(g + 1) * NT, :],
                                      iota_p[:, :].unsqueeze(1).to_broadcast([P, NT, P]),
                                      place[:, t].unsqueeze(2).to_broadcast([P, NT, P]), ALU.is_equal
                                      ).then_inc(s_hotf, 1)

            pass_no, = counters(dve, "results_wanted")

            def answers(h):
                def one_pass(slots):
                    dve.reg_add(pass_no, pass_no, 1)
                    dve.wait_ge(s_res, pass_no)
                    again(dve.tensor_scalar(f_res[:, 0, :], bank(4)[0:1, 0:2 * GS], b_out[:, 0:1], MAGIC, ALU.add, ALU.add))
                    again(dve.tensor_scalar(f_res[:, 1, :], f_res[:, 0, :], MAGIC, 0.0, ALU.subtract, ALU.max))
                    again(dve.tensor_scalar(f_res[:, 0, :], f_res[:, 1, :], 15.0, None, ALU.min))
                    again(dve.scalar_tensor_tensor(answer[:, slots], f_res[:, 0, GS:2 * GS], 16.0,
                                                   f_res[:, 0, 0:GS], ALU.mult, ALU.add))
                    dve.memset(f_res[:, 1, 0:1], 0.0).then_inc(s_rese, 1)

                one_pass(slice(0, GS))
                dve.reg_load(go, active[0:1, h, 1:2])
                with dve.If_ne(go, 0):
                    with dve.Fori(1, PASSES) as g:
                        dve.reg_load(go, active[0:1, h, bass.ds(g, 1)])
                        with dve.If_ne(go, 0):
                            one_pass(bass.ds(g * GS, GS))
                dve.memset(f_res[:, 1, 1:2], 0.0).then_inc(s_quarter, 1)

            def add_hots(h):
                for half in range(QT // NH):
                    k = h * (QT // NH) + half
                    t = slice(k * NH, (k + 1) * NH)
                    for g in range(NH // NT):
                        dve.wait_ge(s_sp, k * (NH // NT) + g + 1)
                        for i in range(NT):
                            n = k * NH + g * NT + i
                            last = dve.scalar_tensor_tensor(junk_b[:, i * P:(i + 1) * P], iota_p[:, :], place[:, n:n + 1],
                                                            bank(6)[:, i * P:(i + 1) * P], ALU.is_equal, ALU.mult,
                                                            accum_out=f_both[:, g * NT + i:g * NT + i + 1])
                        last.then_inc(s_spe, 1)
                    dve.wait_ge(s_spe, (k + 1) * (NH // NT))
                    done(dve.tensor_copy(f_both_i[:, 0, :], f_both[:, :]))
                    dve.tensor_scalar(f_both_i[:, 1, :], f_both_i[:, 0, :], 15, None, ALU.bitwise_and)
                    dve.tensor_scalar(f_twice[:, :], marked[:, t], 2.0, None, ALU.mult)
                    done(dve.tensor_scalar(f_both_i[:, 2, :], f_both_i[:, 0, :], 4, None, ALU.arith_shift_right))
                    done(dve.tensor_copy(f_pair.rearrange("p t s -> p s t"), f_both_i[:, 1:3, :]))
                    done(dve.tensor_tensor(hot.rearrange("p t s j -> p (t s) j"),
                                           iota_p[:, 0:16].unsqueeze(1).to_broadcast([P, 2 * NH, 16]),
                                           f_pair.rearrange("p t s -> p (t s)").unsqueeze(2).to_broadcast([P, 2 * NH, 16]),
                                           ALU.is_equal))
                    done(dve.tensor_tensor(hot.rearrange("p t s j -> p t (s j)"), hot.rearrange("p t s j -> p t (s j)"),
                                           f_twice[:, :].unsqueeze(2).to_broadcast([P, NH, 32]), ALU.mult))
                    dve.wait_ge(s_y, (k + 1) * NH)
                    dve.tensor_tensor(x1[:, t, OUT0:OUT0 + 32], x1[:, t, OUT0:OUT0 + 32],
                                      hot.rearrange("p t s j -> p t (s j)"), ALU.add).then_inc(s_hot, 1)
                    dve.wait_ge(s_hot, k + 1)

            normalise(dve, 0)
            find_features(0)
            place_quarter(0)
            slot_hots(0)
            find_features(1)
            for h in range(QUARTERS):
                if h + 1 < QUARTERS:
                    place_quarter(h + 1)
                    slot_hots(h + 1)
                if h:
                    add_hots(h - 1)
                if h + 2 < QUARTERS:
                    find_features(h + 2)
                answers(h)
            add_hots(QUARTERS - 1)

        @block.tensor
        def _(pe):
            pe.wait_ge(s_const, 8)
            pe.wait_ge(s_cnt, SPLIT + 1)
            pe.matmul(bank(6)[0:T, 0:1], count[:, :], ones[:, 0:1], start=True, stop=True).then_inc(s_tot, 1)
            pe.wait_ge(s_nch, 1)
            pe.matmul(bank(6)[0:T, 64:65], before[0:T, 0:T], n_chunks[:, 0:1], start=True, stop=True)
            pe.matmul(bank(6)[0:1, 128:129], n_chunks[:, 0:1], ones[0:T, 0:1], start=True, stop=True).then_inc(s_first, 1)
            pe.wait_ge(s_diag, 1)
            pe.matmul(bank(7)[:, 0:T], before[:, :], count[:, :], start=True, stop=False)
            pe.matmul(bank(7)[:, 0:T], ones[0:T, :], first_diag[:, :], start=False, stop=True).then_inc(s_base, 1)
            pe.wait_ge(s_isf, 1)
            for c in range(0, CHUNKS, D):
                e = min(CHUNKS, c + D)
                last = pe.matmul(psum[0:1, c:e], ones[0:T, 0:1], is_first[:, c:e], start=True, stop=True)
            last.then_inc(s_flagm, 1)
            pe.wait_ge(s_flags, 1)
            pe.wait_ge(s_w, 16)
            for k in range(KD):
                for j in range(KD):
                    last = pe.transpose(bank(k)[:, j * P:(j + 1) * P], w_load[:, j, k * P:(k + 1) * P], ident[:, :])
                last.then_inc(s_wtr, 1)
            pe.wait_ge(s_wev, KD)
            with pe.Fori(0, T) as n:
                pe.wait_ge(s_xn, n + 1)
                for k in range(KD):
                    last = pe.transpose(bank(4)[:, k * P:(k + 1) * P], xn[:, k * P:(k + 1) * P], ident[:, :])
                last.then_inc(s_tr, 1)
                pe.wait_ge(s_tev, n + 1)
                for k in range(KD):
                    last = pe.matmul(bank(5), xnT[:, k, :], wT[:, k, :], start=(k == 0), stop=(k == KD - 1))
                last.then_inc(s_mm, 1)
            pe.wait_ge(s_hev, T)
            pe.matmul(bank(0), ident[:, :], x1[:, 0, :], start=True, stop=False, skip_group_check=True
                      ).then_inc(s_done, PART)
            with ExitStack() as regs:
                mark = [regs.enter_context(pe.register(f"pmark{k}")) for k in range(RING)]
                tile = regs.enter_context(pe.register("ptile"))
                at_bank = regs.enter_context(pe.register("pbank"))
                go, = counters(pe, "pe_live")
                pe.reg_mov(tile, 0)
                pe.reg_mov(at_bank, 0)

                def summed():
                    return psum[:, bass.ds(pe.snap(at_bank, min_val=0, max_val=(AGG - 1) * D), D)]

                def one_round(it, r, c):
                    pe.reg_load(mark, flags[0:1, bass.ds(c + LAG, RING)])
                    for k in range(RING):
                        s = k % PART
                        pe.wait_ge(s_op, c + (RING + k + 1))
                        with pe.If_ne(mark[k], 0):
                            pe.reg_add(tile, tile, 1)
                            n = pe.snap(tile, min_val=0, max_val=T - 1)
                            pe.wait_ge(s_aggfree, n + 1)
                            pe.reg_mov(at_bank, (n % AGG) * D)
                            pe.matmul(summed(), ident[:, :], x1[:, bass.ds(n, 1), :].rearrange("p a f -> p (a f)"),
                                      start=True, stop=False, skip_group_check=True)
                        pe.matmul(summed(), onehot[:, s, :], hi[:, s, :], start=False, stop=True,
                                  skip_group_check=True)
                        pe.matmul(summed(), onehot[:, s, :], lo[:, s, :], start=False, stop=True,
                                  skip_group_check=True).then_inc(s_done, 1)
                rounds(pe, go, one_round)
            pe.wait_ge(s_x1, 1)
            pe.wait_ge(s_fw, 32)
            for l in range(LH):
                for d in range(2):
                    for e in range(2):
                        o = l * D + d * G + e * GH
                        last = pe.transpose(psum[0:GH, o:o + GH], fw_load[:, e, l, d * GH:(d + 1) * GH],
                                            ident[0:GH, 0:GH])
            last.then_inc(s_fwt, 1)
            pe.wait_ge(s_fin, 16 * 12)
            pe.wait_ge(s_fb, 16 * 5)
            base = [ctx.enter_context(pe.register(f"pbase{i}")) for i in range(NT)]
            layers, pass_no, single = counters(pe, "layers_done", "passes_done", "pe_alone")

            def rank_quarter(h):
                t = slice(h * QT, (h + 1) * QT)
                pe.wait_ge(s_mark, h + 1)
                if h:
                    pe.wait_ge(s_place, h)
                pe.matmul(bank(7)[:, 0:QT], before[:, :], marked[:, t], start=True, stop=True)
                pe.matmul(bank(7)[:, QT:2 * QT], ones[:, :], marked[:, t], start=True, stop=True).then_inc(s_rank2, 1)

            def pack_tiles(h, g):
                k = h * GROUPS + g
                pe.wait_ge(s_hotf, k + 1)
                if k >= 2:
                    pe.wait_ge(s_pke, (k - 1) * NT)
                for i in range(NT):
                    last = pe.matmul(bank(5 + 2 * (g % 2))[0:5, i * P:(i + 1) * P], f_in[:, k * NT + i, :],
                                     slot_hot[:, g * NT + i, :], start=True, stop=True)
                last.then_inc(s_pk, 1)

            def spread_tiles(h, g):
                pe.wait_ge(s_quarter, h + 1)
                pe.reg_load(base, starts[0:1, h, g * NT:(g + 1) * NT])
                at_least(pe, s_spe, h * GROUPS + g)
                for i in range(NT):
                    b = pe.snap(base[i], min_val=0, max_val=SLOTS)
                    last = pe.matmul(bank(6)[:, i * P:(i + 1) * P], ones_b[:, :], answer[:, bass.ds(b, P)],
                                     start=True, stop=True)
                last.then_inc(s_sp, 1)

            def one_pass(slots, between):
                for l in range(L - 1):
                    if l:
                        pe.reg_add(layers, layers, 1)
                    for e in range(2):
                        to = bank(2 * (l % 2) + e)[0:GP, 0:2 * GS]
                        rows = slice(e * GP, (e + 1) * GP)
                        if l == 0:
                            for s in range(2):
                                last = pe.matmul(to[:, s * GS:(s + 1) * GS], fw_in[:, s, rows], packed[:, slots],
                                                 start=True, stop=True)
                        else:
                            for d in range(2):
                                if e == 0:
                                    pe.wait_ge(s_fa[d], layers)
                                last = pe.matmul(to, fwT[:, d, l - 1, rows], act_f[:, (l - 1) % 2, d, :],
                                                 start=(d == 0), stop=(d == 1))
                        last.then_inc(s_fs[e], 1)
                    between(l)
                pe.reg_add(layers, layers, 1)
                pe.reg_add(pass_no, pass_no, 1)
                for d in range(2):
                    pe.wait_ge(s_fa[d], layers)
                pe.wait_ge(s_rese, pass_no)
                for d in range(2):
                    last = pe.matmul(bank(4)[0:1, 0:2 * GS], fw_out[:, d:d + 1], act_f[:, (L - 2) % 2, d, :],
                                     start=(d == 0), stop=(d == 1))
                last.then_inc(s_res, 1)

            rank_quarter(0)
            for g in range(GROUPS):
                pack_tiles(0, g)
            for h in range(QUARTERS):
                pe.wait_ge(s_fwe, LH)
                pe.wait_ge(s_pke, (h + 1) * QT)
                pe.reg_load(single, alone[0:1, h:h + 1])

                def between(l):
                    if l == 0 and h + 1 < QUARTERS:
                        rank_quarter(h + 1)
                    if h and 0 <= l - FIRST_PACK < GROUPS:
                        spread_tiles(h - 1, l - FIRST_PACK)
                    if h + 1 < QUARTERS and 0 <= l - FIRST_PACK < GROUPS:
                        with pe.If_ne(single, 0):
                            pack_tiles(h + 1, l - FIRST_PACK)

                one_pass(slice(0, GS), between)
                pe.reg_load(go, active[0:1, h, 1:2])
                with pe.If_ne(go, 0):
                    with pe.Fori(1, PASSES) as g:
                        pe.reg_load(go, active[0:1, h, bass.ds(g, 1)])
                        with pe.If_ne(go, 0):
                            one_pass(bass.ds(g * GS, GS), lambda l: None)
                    if h + 1 < QUARTERS:
                        for g in range(GROUPS):
                            pack_tiles(h + 1, g)
            for g in range(GROUPS):
                spread_tiles(QUARTERS - 1, g)


_INS = ["x", "src", "dst", "edge_weight", "L0_gnn_weight", "L0_ffn_W", "L0_ffn_b"]


def kernel(**inputs):
    import numpy as _np
    import concourse.bacc as _bacc
    from concourse import mybir as _mybir
    from concourse.bass_utils import run_bass_kernel_spmd as _run

    nc = _bacc.Bacc("TRN2", target_bir_lowering=False, num_devices=1)
    arrays, args = {}, []
    for name in _INS:
        a = _np.ascontiguousarray(inputs[name])
        arrays[f"in_{name}"] = a
        args.append(nc.dram_tensor(f"in_{name}", a.shape, _mybir.dt.from_np(a.dtype), kind="ExternalInput").ap())
    args.append(nc.dram_tensor("out_0", inputs["x"].shape, _mybir.dt.float32, kind="ExternalOutput").ap())
    gnn_ffn(nc, *args)
    r = _run(nc, [arrays], core_ids=[0])
    return r.results[0]["out_0"]
```
